# Optimizing a Trainium2 kernel written in Bass

```python
import numpy as np
import jax
import jax.numpy as jnp

def _softmax(x, axis=-1):
    return jax.nn.softmax(x, axis=axis)

def _gelu(x):
    return jax.nn.gelu(x, approximate=True)

def _silu(x):
    return jax.nn.silu(x)

def _sigmoid(x):
    return jax.nn.sigmoid(x)

def _layernorm(x, axis=-1, eps=1e-05):
    m = jnp.mean(x, axis=axis, keepdims=True)
    v = jnp.var(x, axis=axis, keepdims=True)
    return (x - m) / jnp.sqrt(v + eps)

def _scatter_add(tgt, idx, src, axis=0):
    return tgt.at[idx].add(src)

def _segment_sum(src, seg, n):
    return jax.ops.segment_sum(src, seg, n)
kernel_name = 'mk_decoder_postln_d1_seqx_r8_268561'

def setup_inputs(seed: int=0):
    np.random.seed(seed)
    _w = jnp.asarray

    def _rec_inputs():
        import jax
        import jax.numpy as jnp
        _rk = jax.random.key(seed)
        x = 0.000341 + 1 * jax.random.normal(jax.random.fold_in(_rk, 1), (16, 128, 256), jnp.float32)
        _lenS = 128 - jax.random.randint(jax.random.fold_in(_rk, 7), (16,), 0, max(1, 128 // 4) + 1, jnp.int32)
        _lenS2 = 128 - jax.random.randint(jax.random.fold_in(_rk, 8), (16,), 0, max(1, 128 // 4) + 1, jnp.int32)
        _ctx_2048P = jax.random.normal(jax.random.fold_in(_rk, 11), (16, 16, 256), jnp.float32)
        _ctx_2048c = jax.random.dirichlet(jax.random.fold_in(_rk, 511), 0.3 * jnp.ones((16,), jnp.float32), (16, 128))
        _ctx_2048t = jnp.einsum('bsk,bkd->bsd', _ctx_2048c, _ctx_2048P)
        _ctx_2048t = _ctx_2048t * jax.lax.rsqrt(jnp.mean(jnp.square(_ctx_2048t)) + 1e-12) * 0.953939
        ctx_2048 = -1.47943e-05 + 1.00017 * (_ctx_2048t + 0.3 * jax.random.normal(jax.random.fold_in(_rk, 611), (16, 128, 256), jnp.float32))
        return (x, ctx_2048)
    x, ctx_2048 = _rec_inputs()

    def _L0_attn_setup():
        import jax, jax.numpy as jnp
        import numpy as np
        B, S, D = (2, 256, 256)
        H, KVH = (16, 4)
        HD = D // H
        KVD = KVH * HD
        BASE = 10000.0
        EPS = 1.1920929e-07

        def _rms_norm(t):
            return t * jax.lax.rsqrt(jnp.mean(t * t, axis=-1, keepdims=True) + EPS)

        def _rope_tables(s, dtype):
            inv_freq = 1.0 / BASE ** (jnp.arange(0, HD, 2, dtype=jnp.float32) / HD)
            t = jnp.arange(s, dtype=jnp.float32)
            freqs = jnp.outer(t, inv_freq)
            cos = jnp.cos(freqs)[None, None].astype(dtype)
            sin = jnp.sin(freqs)[None, None].astype(dtype)
            return (cos, sin)

        def _apply_rope(t, cos, sin):
            half = t.shape[-1] // 2
            t1, t2 = (t[..., :half], t[..., half:])
            return jnp.concatenate([t1 * cos + t2 * sin, -t1 * sin + t2 * cos], axis=-1)
        key = jax.random.key(seed)
        ks = jax.random.split(key, 9)
        sd = 1.0 / np.sqrt(D)
        x = jax.random.normal(ks[0], (B, S, D), jnp.float32)
        Wq = jax.random.normal(ks[1], (D, D), jnp.float32) * sd
        bq = jnp.zeros((D,), jnp.float32)
        Wk = jax.random.normal(ks[2], (KVD, D), jnp.float32) * sd
        bk = jnp.zeros((KVD,), jnp.float32)
        Wv = jax.random.normal(ks[3], (KVD, D), jnp.float32) * sd
        bv = jnp.zeros((KVD,), jnp.float32)
        Wo = jax.random.normal(ks[4], (D, D), jnp.float32) * sd
        bo = jnp.zeros((D,), jnp.float32)
        q_gain = jnp.ones((H,), jnp.float32)
        return {'x': x, 'Wq': Wq, 'bq': bq, 'Wk': Wk, 'bk': bk, 'Wv': Wv, 'bv': bv, 'Wo': Wo, 'bo': bo, 'q_gain': q_gain}
    _L0_attn_all = _L0_attn_setup()
    _L0_attn_in = {k: v for k, v in _L0_attn_all.items() if k in ('Wq', 'bq', 'Wk', 'bk', 'Wv', 'bv', 'Wo', 'bo', 'q_gain')}
    del _L0_attn_all

    def _L0_xattn_setup():
        import jax, jax.numpy as jnp
        import numpy as np

        def _wkv(time_decay, time_first, k, v):
            w = -jnp.exp(time_decay)
            u = time_first
            B, T, C = k.shape
            aa = jnp.zeros((B, C), dtype=k.dtype)
            bb = jnp.zeros((B, C), dtype=k.dtype)
            pp = jnp.full((B, C), -1e+38, dtype=k.dtype)

            def step(carry, kv_t):
                aa, bb, pp = carry
                kt, vt = kv_t
                ww = u + kt
                q = jnp.maximum(pp, ww)
                e1 = jnp.exp(pp - q)
                e2 = jnp.exp(ww - q)
                y_t = (e1 * aa + e2 * vt) / (e1 * bb + e2)
                ww2 = pp + w
                q2 = jnp.maximum(ww2, kt)
                e1b = jnp.exp(ww2 - q2)
                e2b = jnp.exp(kt - q2)
                new_carry = (e1b * aa + e2b * vt, e1b * bb + e2b, q2)
                return (new_carry, y_t)
            ks = jnp.transpose(k, (1, 0, 2))
            vs = jnp.transpose(v, (1, 0, 2))
            _, ys = jax.lax.scan(step, (aa, bb, pp), (ks, vs))
            return jnp.transpose(ys, (1, 0, 2))
        key = jax.random.key(seed)
        k1, k2, k3, k4 = jax.random.split(key, 4)
        B, T, C = (8, 128, 256)
        return {'batch_size': B, 'seq_len': T, 'embedding_dim': C, 'time_decay': jax.random.normal(k1, (C,), dtype=jnp.float32), 'time_first': jax.random.normal(k2, (C,), dtype=jnp.float32), 'k': jax.random.normal(k3, (B, T, C), dtype=jnp.float32), 'v': jax.random.normal(k4, (B, T, C), dtype=jnp.float32)}
    _L0_xattn_all = _L0_xattn_setup()
    _L0_xattn_in = {k: v for k, v in _L0_xattn_all.items() if k in ('time_decay', 'time_first')}
    del _L0_xattn_all

    def _L0_ffn_setup():
        import jax, jax.numpy as jnp
        import numpy as np

        @jax.custom_vjp
        def ste_sign(x):
            return jnp.sign(x)

        def _ste_fwd(x):
            return (jnp.sign(x), None)

        def _ste_bwd(_, g):
            return (g,)
        ste_sign.defvjp(_ste_fwd, _ste_bwd)
        D_MODEL = 256
        D_HIDDEN = 1024
        key = jax.random.key(seed)
        k_x, k_up, k_dn = jax.random.split(key, 3)
        x = jax.random.normal(k_x, (2, 256, D_MODEL), dtype=jnp.float32)
        up_weight = jax.random.normal(k_up, (D_HIDDEN, D_MODEL), dtype=jnp.float32) * 0.02
        down_weight = jax.random.normal(k_dn, (D_MODEL, D_HIDDEN), dtype=jnp.float32) * 0.02
        up_scale = jnp.ones((D_HIDDEN,), dtype=jnp.float32)
        down_scale = jnp.ones((D_MODEL,), dtype=jnp.float32)
        output_scale = jnp.ones((1,), dtype=jnp.float32)
        return {'x': x, 'up_weight': up_weight, 'down_weight': down_weight, 'up_scale': up_scale, 'down_scale': down_scale, 'output_scale': output_scale}
    _L0_ffn_all = _L0_ffn_setup()
    _L0_ffn_in = {k: v for k, v in _L0_ffn_all.items() if k in ('up_weight', 'down_weight', 'up_scale', 'down_scale', 'output_scale')}
    del _L0_ffn_all
    return {'x': x, 'ctx_2048': ctx_2048, 'L0_attn_Wq': _L0_attn_in['Wq'], 'L0_attn_bq': _L0_attn_in['bq'], 'L0_attn_Wk': _L0_attn_in['Wk'], 'L0_attn_bk': _L0_attn_in['bk'], 'L0_attn_Wv': _L0_attn_in['Wv'], 'L0_attn_bv': _L0_attn_in['bv'], 'L0_attn_Wo': _L0_attn_in['Wo'], 'L0_attn_bo': _L0_attn_in['bo'], 'L0_attn_q_gain': _L0_attn_in['q_gain'], 'L0_xattn_time_decay': _L0_xattn_in['time_decay'], 'L0_xattn_time_first': _L0_xattn_in['time_first'], 'L0_ffn_up_weight': _L0_ffn_in['up_weight'], 'L0_ffn_down_weight': _L0_ffn_in['down_weight'], 'L0_ffn_up_scale': _L0_ffn_in['up_scale'], 'L0_ffn_down_scale': _L0_ffn_in['down_scale'], 'L0_ffn_output_scale': _L0_ffn_in['output_scale']}

def reference(x, ctx_2048, L0_attn_Wq, L0_attn_bq, L0_attn_Wk, L0_attn_bk, L0_attn_Wv, L0_attn_bv, L0_attn_Wo, L0_attn_bo, L0_attn_q_gain, L0_xattn_time_decay, L0_xattn_time_first, L0_ffn_up_weight, L0_ffn_down_weight, L0_ffn_up_scale, L0_ffn_down_scale, L0_ffn_output_scale):
    import jax
    import jax.numpy as jnp

    def _L0_attn_ref(x, Wq, bq, Wk, bk, Wv, bv, Wo, bo, q_gain):
        import jax, jax.numpy as jnp
        import numpy as np
        B, S, D = (2, 256, 256)
        H, KVH = (16, 4)
        HD = D // H
        KVD = KVH * HD
        BASE = 10000.0
        EPS = 1.1920929e-07

        def _rms_norm(t):
            return t * jax.lax.rsqrt(jnp.mean(t * t, axis=-1, keepdims=True) + EPS)

        def _rope_tables(s, dtype):
            inv_freq = 1.0 / BASE ** (jnp.arange(0, HD, 2, dtype=jnp.float32) / HD)
            t = jnp.arange(s, dtype=jnp.float32)
            freqs = jnp.outer(t, inv_freq)
            cos = jnp.cos(freqs)[None, None].astype(dtype)
            sin = jnp.sin(freqs)[None, None].astype(dtype)
            return (cos, sin)

        def _apply_rope(t, cos, sin):
            half = t.shape[-1] // 2
            t1, t2 = (t[..., :half], t[..., half:])
            return jnp.concatenate([t1 * cos + t2 * sin, -t1 * sin + t2 * cos], axis=-1)
        b, s, d = x.shape
        q = (jnp.einsum('bsd,ed->bse', x, Wq) + bq).reshape(b, s, H, HD).transpose(0, 2, 1, 3)
        k = (jnp.einsum('bsd,ed->bse', x, Wk) + bk).reshape(b, s, KVH, HD).transpose(0, 2, 1, 3)
        v = (jnp.einsum('bsd,ed->bse', x, Wv) + bv).reshape(b, s, KVH, HD).transpose(0, 2, 1, 3)
        q = _rms_norm(q)
        k = _rms_norm(k)
        cos, sin = _rope_tables(s, q.dtype)
        q = _apply_rope(q, cos, sin)
        k = _apply_rope(k, cos, sin)
        q = q * q_gain[None, :, None, None]
        rep = H // KVH
        k = jnp.repeat(k, rep, axis=1)
        v = jnp.repeat(v, rep, axis=1)
        scale = HD ** (-0.5)
        attn = jnp.einsum('bhqd,bhkd->bhqk', q * scale, k)
        causal = jnp.tril(jnp.ones((s, s), dtype=bool))
        attn = jnp.where(causal[None, None], attn, -jnp.inf)
        attn = jax.nn.softmax(attn, axis=-1)
        out = jnp.einsum('bhqk,bhkd->bqhd', attn, v).reshape(b, s, d)
        return jnp.einsum('bsd,ed->bse', out, Wo) + bo

    def _L0_xattn_ref(batch_size, seq_len, embedding_dim, time_decay, time_first, k, v):
        import jax, jax.numpy as jnp
        import numpy as np

        def _wkv(time_decay, time_first, k, v):
            w = -jnp.exp(time_decay)
            u = time_first
            B, T, C = k.shape
            aa = jnp.zeros((B, C), dtype=k.dtype)
            bb = jnp.zeros((B, C), dtype=k.dtype)
            pp = jnp.full((B, C), -1e+38, dtype=k.dtype)

            def step(carry, kv_t):
                aa, bb, pp = carry
                kt, vt = kv_t
                ww = u + kt
                q = jnp.maximum(pp, ww)
                e1 = jnp.exp(pp - q)
                e2 = jnp.exp(ww - q)
                y_t = (e1 * aa + e2 * vt) / (e1 * bb + e2)
                ww2 = pp + w
                q2 = jnp.maximum(ww2, kt)
                e1b = jnp.exp(ww2 - q2)
                e2b = jnp.exp(kt - q2)
                new_carry = (e1b * aa + e2b * vt, e1b * bb + e2b, q2)
                return (new_carry, y_t)
            ks = jnp.transpose(k, (1, 0, 2))
            vs = jnp.transpose(v, (1, 0, 2))
            _, ys = jax.lax.scan(step, (aa, bb, pp), (ks, vs))
            return jnp.transpose(ys, (1, 0, 2))
        assert seq_len <= 128
        return _wkv(time_decay, time_first, k, v)

    def _L0_ffn_ref(x, up_weight, down_weight, up_scale, down_scale, output_scale):
        import jax, jax.numpy as jnp
        import numpy as np

        @jax.custom_vjp
        def ste_sign(x):
            return jnp.sign(x)

        def _ste_fwd(x):
            return (jnp.sign(x), None)

        def _ste_bwd(_, g):
            return (g,)
        ste_sign.defvjp(_ste_fwd, _ste_bwd)
        D_MODEL = 256
        D_HIDDEN = 1024
        up_w = ste_sign(up_weight)
        down_w = ste_sign(down_weight)
        hidden = jnp.einsum('bsd,hd->bsh', x, up_w) * up_scale
        hidden = jax.nn.relu(hidden)
        out = jnp.einsum('bsh,dh->bsd', hidden, down_w) * down_scale
        return out * output_scale
    x = _layernorm(x + _L0_attn_ref(x, L0_attn_Wq, L0_attn_bq, L0_attn_Wk, L0_attn_bk, L0_attn_Wv, L0_attn_bv, L0_attn_Wo, L0_attn_bo, L0_attn_q_gain), axis=-1)
    x = _layernorm(x + _L0_xattn_ref(16, 128, 256, L0_xattn_time_decay, L0_xattn_time_first, x, ctx_2048), axis=-1)
    x = _layernorm(x + _L0_ffn_ref(x, L0_ffn_up_weight, L0_ffn_down_weight, L0_ffn_up_scale, L0_ffn_down_scale, L0_ffn_output_scale), axis=-1)
    return x

_drawn_inputs = setup_inputs


def setup_inputs(seed=0):
    import zlib

    import numpy as np

    out = dict(_drawn_inputs(seed))
    spreads = {'L0_attn_bq': (0.0, 0.471),
     'L0_attn_bk': (0.0, 0.634),
     'L0_attn_bv': (0.0, 0.1),
     'L0_attn_bo': (0.0, 0.1),
     'L0_attn_q_gain': (1.0, 0.2),
     'L0_ffn_up_scale': (1.0, 0.2),
     'L0_ffn_down_scale': (1.0, 0.2)}
    factors = {}
    for name, (base, spread) in spreads.items():
        noise = np.random.default_rng([zlib.crc32(name.encode()), seed]).standard_normal(out[name].shape)
        drawn = base * np.exp(spread * noise) if base else spread * noise
        out[name] = jnp.asarray(drawn.astype(out[name].dtype))
    for name, factor in factors.items():
        out[name] = (out[name] * factor).astype(out[name].dtype)
    return out
```

```python
from contextlib import ExitStack

import numpy as np

import concourse.bass as bass
from concourse import mybir

ALU = mybir.AluOpType
ACT = mybir.ActivationFunctionType
F32 = mybir.dt.float32
F16 = mybir.dt.float16
BF16 = mybir.dt.bfloat16
I32 = mybir.dt.int32
AX_X = mybir.AxisListType.X

B, S, D = 16, 128, 256
H, KVH = 16, 4
HD = D // H
KVD = KVH * HD
NQK = H + KVH
DFF = 1024
T = 2
PAIRS = B // T
NC = D // 128
NJ = DFF // 128
E = D + 2 * KVD
REP = H // KVH
BLOCKS = NQK // 2
QBLOCKS = H // 2
RMS_EPS = 1.1920929e-07
LN_EPS = 1e-5
LN_MAX = float(D) ** 0.5
MASKED = -1e38
DEPTH = 3


def first(p):
    return isinstance(p, int) and p == 0


def active(p):
    return not isinstance(p, int) or 0 <= p < PAIRS


def build(nc, x, xT, ctxT, wqkv, bqkv, gains, wo, bo, decay_in, first_in, up, down, up_s, down_s, out_s,
          rope_cos, rope_sin, mask_in, ident_in, out):
    with ExitStack() as ctx:
        def sb(name, shape, dt=F32):
            return ctx.enter_context(nc.sbuf_tensor(name, shape, dt))

        def sem(name):
            return ctx.enter_context(nc.semaphore(name))

        bank = [ctx.enter_context(nc.psum_tensor(f"bank{n}", [128, 512], F32)) for n in range(8)]
        ring = [bank[6], bank[7]]

        wqkv_sb = sb("wqkv_sb", [128, NC, E])
        wo_sb = sb("wo_sb", [128, NC, D])
        bqk_b = sb("bqk_b", [128, E])
        gain_in = sb("gain_in", [128, T, H])
        gain_b = sb("gain_b", [128, T, NQK])
        bo_b = sb("bo_b", [128, D])
        dsc_b = sb("dsc_b", [128, D])
        osc_b = sb("osc_b", [128, 1])
        cos_sb = sb("cos_sb", [128, HD])
        sin_sb = sb("sin_sb", [128, HD])
        mask_f = sb("mask_f", [128, 128])
        mask_bf = sb("mask_bf", [128, REP, 128], BF16)
        id_f = sb("id_f", [128, 128])
        id_h = sb("id_h", [128, 128], F16)
        id_b = sb("id_b", [128, 128], BF16)
        up_f = sb("up_f", [128, NC, DFF])
        up_sb = sb("up_sb", [128, NC, DFF], F16)
        dn_f = sb("dn_f", [128, NJ, D])
        dn_sb = sb("dn_sb", [128, NJ, D], BF16)
        ups_sb = sb("ups_sb", [128, NJ])
        ups_pow = sb("ups_pow", [128, NJ])
        ups_man = sb("ups_man", [128, NJ])
        tdec = sb("tdec", [128, NC])
        tdec2 = sb("tdec2", [128, NC])
        tfirst = sb("tfirst", [128, NC])
        e_state = sb("e_state", [128, NC])
        e_now = sb("e_now", [128, NC])
        u_neg = sb("u_neg", [128, NC])
        u_pos = sb("u_pos", [128, NC])
        dec_sb = sb("dec_sb", [128, 2, NC, T, S])
        half_neg = sb("half_neg", [128, T * NQK])
        ln_max = sb("ln_max", [128, 1])

        xT_sb = sb("xT_sb", [128, NC, T, S])
        x_sb = sb("x_sb", [128, T, D])
        ctxT_sb = sb("ctxT_sb", [128, NC, T, S])
        xb_sb = sb("xb_sb", [128, T, D])
        qk = sb("qk", [128, T * NQK, HD])
        v_sb = sb("v_sb", [128, T, KVH, HD + 1])
        sq = sb("sq", [128, T * NQK, HD])
        ssum = sb("ssum", [128, T * NQK])
        msq = sb("msq", [128, T * NQK])
        rinv = sb("rinv", [128, T * NQK])
        rscale = sb("rscale", [128, T * NQK])
        rope_a = sb("rope_a", [128, T * NQK, HD])
        rope_b = sb("rope_b", [128, T * NQK, HD])
        rot = sb("rot", [128, T * NQK, HD])
        qn = sb("qn", [128, T * NQK, HD])
        stack = sb("stack", [128, T, NQK, 4, HD], F16)
        qT_sb = sb("qT_sb", [128, T, QBLOCKS, 128], F16)
        kT_sb = sb("kT_sb", [128, T, 2, 128], F16)
        probs = sb("probs", [128, KVH, REP, 128])
        prec = sb("prec", [128, T, H])
        att = sb("att", [128, T, H, HD])
        attT_sb = sb("attT_sb", [128, NC, T, 128])
        r1 = sb("r1", [128, T, D])
        x1 = sb("x1", [128, T, D])
        stats = [sb(f"stats{n}", [128, T, 6]) for n in range(3)]
        mv = [sb(f"mv{n}", [128, T, 2]) for n in range(3)]
        veps = [sb(f"veps{n}", [128, T]) for n in range(3)]
        rstd = [sb(f"rstd{n}", [128, T]) for n in range(3)]
        ke = sb("ke", [128, 2, NC, T, S])
        state = sb("state", [128, 2 * NC * T * S + 2])
        now = sb("now", [128, 2, NC, T, S])
        ratio = sb("ratio", [128, 2, NC, T, S])
        lnden = sb("lnden", [128, NC, T, S])
        rec0 = sb("rec0", [128, NC, T, S])
        newt = sb("newt", [128, NC, T, S])
        nrec = sb("nrec", [128, NC, T, S])
        ny = sb("ny", [128, NC, T, S])
        zT = sb("zT", [128, NC, T, S])
        x2 = sb("x2", [128, T, D])
        x2_keep = sb("x2_keep", [128, T, D])
        x2hi = sb("x2hi", [128, NC, T, S], F16)
        x2lo = sb("x2lo", [128, NC, T, S], F16)
        hid = sb("hid", [128, NJ, T * S])
        hid_hi = sb("hid_hi", [128, NJ, T * S], F16)
        hid_lo = sb("hid_lo", [128, NJ, T * S], F16)
        o3 = sb("o3", [128, T, D])
        r3 = sb("r3", [128, T, D])
        outb = sb("outb", [128, T, D])

        names = dict(
            xT_in=16, x_in=16, ctx_in=16, stored=16,
            qkv_mm=2, kT_tr=1, qT_tr=2, scores_mm=8, pv_mm=8, attT_tr=1, wo_mm=1, x1T_tr=1, zT_tr=1,
            x2T_tr=1, up_mm=4, dn_mm=1,
            qkv_out=2, sq_done=1, ssum_done=1, msq_done=1, rinv_done=1, rscale_done=1, rope_done=3,
            rot_done=1, qn_done=1, hi_done=1, lo_done=1, stack_done=3, kT_out=1, q0_out=1, q1_out=1,
            probs_done=8, prec_done=2, att_done=2, attT_out=1, xb_done=1, r1_done=1, bn1=2, ag1=2, ve1=1,
            rs1=1, x1_done=2, ek_done=2, kv_done=1, now_done=2, scan_done=1, fix_done=1, ratio_done=2,
            ln_done=1, rec0_done=1, newt_done=1, nrec_done=1, ny_done=1, z_done=1, bn2=2, ag2=2, ve2=1,
            rs2=1, x2_done=2, kept=1, x2hi_done=1, x2lo_done=1, hid_done=8, hidhi_done=4, hidlo_done=4,
            o3_done=1, r3_done=1, bn3=2, ag3=2, ve3=1, rs3=1, out_done=2)
        sems = {n: sem(n) for n in names}
        params_in = sem("params_in")
        signs_done = sem("signs_done")
        consts_done = sem("consts_done")
        setup_dve = sem("setup_dve")
        setup_act = sem("setup_act")

        def done(eng, name, p, k=None):
            eng.wait_ge(sems[name], p * names[name] + (names[name] if k is None else k))

        def freed(eng, name, p, back=1, k=None):
            if not (isinstance(p, int) and p < back):
                done(eng, name, p - back, k)

        def alone(eng):
            eng.nop(nofuse=True)

        consts = [(wqkv_sb[:], wqkv), (wo_sb[:], wo), (id_f[:], ident_in), (mask_f[:], mask_in),
                  (cos_sb[:], rope_cos), (sin_sb[:], rope_sin),
                  (bqk_b[:], bqkv.partition_broadcast(128)), (bo_b[:], bo.partition_broadcast(128)),
                  (gain_in[:, 0, :], gains.partition_broadcast(128)), (gain_in[:, 1, :], gains.partition_broadcast(128)),
                  (dsc_b[:], down_s.partition_broadcast(128)), (osc_b[:], out_s.partition_broadcast(128)),
                  (tdec[:], decay_in), (tfirst[:], first_in), (ups_sb[:], up_s),
                  (up_f[:], up), (dn_f[:], down)]
        PARAMS = 16 * len(consts)

        block = ctx.enter_context(nc.Block())

        def pipeline(eng, step, last_extra=0):
            for i in range(DEPTH):
                step(i)
            with eng.Fori(DEPTH, PAIRS) as i:
                step(i)
            for i in range(PAIRS, PAIRS + DEPTH):
                step(i)

        @block.sync
        def _(sp):
            sp.dma_start(xT_sb[:], xT[0]).then_inc(sems["xT_in"], 16)
            for dst, src in consts:
                sp.dma_start(dst, src).then_inc(params_in, 16)
            sp.dma_start(x_sb[:], x[0]).then_inc(sems["x_in"], 16)
            sp.dma_start(ctxT_sb[:], ctxT[0]).then_inc(sems["ctx_in"], 16)

            def step(i):
                if not isinstance(i, int) or i + 1 < PAIRS:
                    done(sp, "qkv_mm", i)
                    sp.dma_start(xT_sb[:], xT[i + 1]).then_inc(sems["xT_in"], 16)
                if not isinstance(i, int) or 1 <= i < PAIRS:
                    done(sp, "xb_done", i - 1)
                    sp.dma_start(x_sb[:], x[i]).then_inc(sems["x_in"], 16)
                    done(sp, "kv_done", i - 1)
                    sp.dma_start(ctxT_sb[:], ctxT[i]).then_inc(sems["ctx_in"], 16)
                if active(i - 3):
                    done(sp, "out_done", i - 3)
                    sp.dma_start(out[i - 3], outb[:]).then_inc(sems["stored"], 16)

            for i in range(DEPTH):
                step(i)
            with sp.Fori(DEPTH, PAIRS - 1) as i:
                step(i)
            for i in range(PAIRS - 1, PAIRS + DEPTH):
                step(i)
            sp.wait_ge(sems["stored"], 16 * PAIRS)

        @block.tensor
        def _(pe):
            pe.wait_ge(params_in, PARAMS)
            pe.wait_ge(consts_done, 6)

            def heads_to_rows(p):
                done(pe, "stack_done", p)
                freed(pe, "r1_done", p)
                for t in range(T):
                    for b in range(2):
                        mm = nc.tensor.transpose(bank[2].bitcast(F16)[:, (2 * t + b) * 128:(2 * t + b + 1) * 128],
                                                 stack[:, t, H + 2 * b:H + 2 * b + 2, :, :].rearrange("p h r d -> p (h r d)"),
                                                 id_h[:])
                mm.then_inc(sems["kT_tr"], 1)
                freed(pe, "x2_done", p, 2)
                for t in range(T):
                    for b in range(QBLOCKS):
                        mm = nc.tensor.transpose(bank[3 * t].bitcast(F16)[:, b * 128:(b + 1) * 128],
                                                 stack[:, t, 2 * b:2 * b + 2, :, :].rearrange("p h r d -> p (h r d)"),
                                                 id_h[:])
                    mm.then_inc(sems["qT_tr"], 1)

            def attend(p, t):
                for g in range(KVH + 1):
                    if g < KVH:
                        n = t * KVH + g
                        if n == 0:
                            done(pe, "kT_out", p)
                            freed(pe, "hid_done", p, 3)
                        if g == 0:
                            done(pe, f"q{t}_out", p)
                        if n >= 2:
                            done(pe, "probs_done", p, n - 1)
                        r = 64 * (g % 2)
                        dst = ring[n % 2]
                        nc.tensor.matmul(dst[:], id_b[:], mask_bf[:].rearrange("p a b -> p (a b)"), start=True, stop=False)
                        nc.tensor.matmul(dst[:], kT_sb[r:r + 64, t, g // 2, :],
                                         qT_sb[r:r + 64, t, 4 * (g // 2):4 * (g // 2) + 4, :].rearrange("p a b -> p (a b)"),
                                         start=False, stop=True).then_inc(sems["scores_mm"], 1)
                    if g >= 1:
                        n = t * KVH + g - 1
                        if g == 1:
                            if t == 0:
                                freed(pe, "x2lo_done", p, 2)
                        done(pe, "probs_done", p, n + 1)
                        for j in range(REP):
                            h = REP * (g - 1) + j
                            mm = nc.tensor.matmul(bank[4 - 2 * t][:, h * (HD + 1):(h + 1) * (HD + 1)],
                                                  probs[:, g - 1, j, :], v_sb[:, t, g - 1, :], start=True, stop=True)
                        mm.then_inc(sems["pv_mm"], 1)

            def project(p):
                done(pe, "xT_in", p)
                for t in range(T):
                    if not first(p):
                        done(pe, f"q{t}_out", p - 1)
                    for c in range(NC):
                        mm = nc.tensor.matmul(bank[3 * t][:, 0:E], xT_sb[:, c, t, :], wqkv_sb[:, c, :],
                                              start=(c == 0), stop=(c == NC - 1))
                    mm.then_inc(sems["qkv_mm"], 1)

            def project_out(p):
                done(pe, "att_done", p)
                a = att[:].rearrange("p t h d -> p t (h d)")
                for c in range(NC):
                    for t in range(T):
                        mm = nc.tensor.transpose(bank[4][:, (2 * c + t) * 128:(2 * c + t + 1) * 128],
                                                 a[:, t, c * 128:(c + 1) * 128], id_f[:])
                mm.then_inc(sems["attT_tr"], 1)
                done(pe, "attT_out", p)
                for t in range(T):
                    for c in range(NC):
                        mm = nc.tensor.matmul(bank[2][:, t * D:(t + 1) * D], attT_sb[:, c, t, :], wo_sb[:, c, :],
                                              start=(c == 0), stop=(c == NC - 1))
                mm.then_inc(sems["wo_mm"], 1)

            def mixed_to_tokens(p, i):
                done(pe, "z_done", p)
                if active(i):
                    done(pe, "qkv_out", i)
                elif active(i - 1):
                    done(pe, "q0_out", i - 1)
                for t in range(T):
                    for c in range(NC):
                        mm = nc.tensor.transpose(bank[0][:, t * D + c * 128:t * D + (c + 1) * 128], zT[:, c, t, :], id_f[:])
                mm.then_inc(sems["zT_tr"], 1)

            def ffn_up(p, i):
                done(pe, "x2hi_done", p)
                done(pe, "x2lo_done", p)
                for n in range(NJ // 2):
                    if n < 2:
                        if active(i - 1):
                            done(pe, "probs_done", i - 1)
                        else:
                            freed(pe, "hid_done", p)
                    else:
                        done(pe, "hid_done", p, 2 * (n - 1))
                    for s in range(2):
                        j = 2 * n + s
                        m = 0
                        for c in range(NC):
                            for part in (x2hi, x2lo):
                                mm = nc.tensor.matmul(ring[n % 2][:, s * T * S:(s + 1) * T * S],
                                                      up_sb[:, c, j * 128:(j + 1) * 128],
                                                      part[:, c, :, :].rearrange("p t s -> p (t s)"),
                                                      start=(m == 0), stop=(m == 2 * NC - 1))
                                m += 1
                    mm.then_inc(sems["up_mm"], 1)

            def x1_to_channels(p):
                done(pe, "x1_done", p)
                freed(pe, "z_done", p)
                for c in range(NC):
                    for t in range(T):
                        mm = nc.tensor.transpose(bank[5][:, (2 * c + t) * 128:(2 * c + t + 1) * 128],
                                                 x1[:, t, c * 128:(c + 1) * 128], id_f[:])
                mm.then_inc(sems["x1T_tr"], 1)

            def x2_to_channels(p, i):
                done(pe, "x2_done", p)
                if active(i - 1):
                    done(pe, "attT_out", i - 1)
                else:
                    freed(pe, "x2lo_done", p)
                for c in range(NC):
                    for t in range(T):
                        mm = nc.tensor.transpose(bank[4][:, (2 * c + t) * 128:(2 * c + t + 1) * 128],
                                                 x2[:, t, c * 128:(c + 1) * 128], id_f[:])
                mm.then_inc(sems["x2T_tr"], 1)

            def ffn_down(p):
                freed(pe, "o3_done", p)
                for t in range(T):
                    for j in range(NJ):
                        if t == 0 and j % 2 == 0:
                            done(pe, "hidhi_done", p, j // 2 + 1)
                            done(pe, "hidlo_done", p, j // 2 + 1)
                        for m, part in enumerate((hid_hi, hid_lo)):
                            mm = nc.tensor.matmul(bank[1][:, t * D:(t + 1) * D], part[:, j, t * S:(t + 1) * S],
                                                  dn_sb[:, j, :], start=(j == 0 and m == 0),
                                                  stop=(j == NJ - 1 and m == 1))
                mm.then_inc(sems["dn_mm"], 1)

            def step(i):
                if active(i - 1):
                    heads_to_rows(i - 1)
                    for t in range(T):
                        attend(i - 1, t)
                if active(i):
                    project(i)
                if active(i - 1):
                    project_out(i - 1)
                if active(i - 2):
                    mixed_to_tokens(i - 2, i)
                if active(i - 3):
                    ffn_up(i - 3, i)
                if active(i - 1):
                    x1_to_channels(i - 1)
                if active(i - 2):
                    x2_to_channels(i - 2, i)
                if active(i - 3):
                    ffn_down(i - 3)

            pipeline(pe, step)

        @block.scalar
        def _(act):
            act.wait_ge(params_in, PARAMS)
            nc.scalar.activation(tdec2[:], tdec[:], ACT.Exp).then_inc(setup_act, 1)
            act.wait_ge(setup_act, 1)
            nc.scalar.activation(tdec[:], tdec2[:], ACT.Exp, scale=-1.0).then_inc(setup_act, 1)
            act.wait_ge(setup_dve, 2)
            nc.scalar.activation(e_state[:], u_pos[:], ACT.Exp, scale=-1.0).then_inc(setup_act, 1)
            nc.scalar.activation(e_now[:], u_neg[:], ACT.Exp).then_inc(setup_act, 1)
            nc.scalar.activation(up_sb[:], up_f[:], ACT.Sign).then_inc(signs_done, 1)
            nc.scalar.activation(dn_f[:], dn_f[:], ACT.Sign).then_inc(setup_act, 1)

            def to_rows(p):
                done(act, "kT_tr", p)
                freed(act, "scores_mm", p)
                nc.scalar.activation(kT_sb[:], bank[2].bitcast(F16)[:, 0:512].rearrange("p (t b s) -> p t b s", t=T, b=2),
                                     ACT.Copy).then_inc(sems["kT_out"], 1)
                done(act, "qT_tr", p, 1)
                nc.scalar.activation(qT_sb[:, 0], bank[0].bitcast(F16)[:].rearrange("p (b s) -> p b s", b=QBLOCKS),
                                     ACT.Copy).then_inc(sems["q0_out"], 1)

            def exps(p, t):
                for g in range(KVH):
                    n = t * KVH + g
                    done(act, "scores_mm", p, n + 1)
                    if n >= KVH:
                        done(act, "pv_mm", p, n - KVH + 1)
                    else:
                        freed(act, "pv_mm", p, k=n + KVH + 1)
                    nc.scalar.activation(probs[:, g].rearrange("p a b -> p (a b)"), ring[n % 2][:], ACT.Exp)\
                        .then_inc(sems["probs_done"], 1)

            def reciprocal_guess(p):
                done(act, "ratio_done", p)
                nc.scalar.activation(lnden[:], ratio[:, 1], ACT.Ln).then_inc(sems["ln_done"], 1)
                done(act, "ln_done", p)
                freed(act, "nrec_done", p)
                nc.scalar.activation(rec0[:], lnden[:], ACT.Exp, scale=-1.0).then_inc(sems["rec0_done"], 1)

            def relu(p, half):
                if half == 0:
                    freed(act, "hidhi_done", p)
                    freed(act, "hidlo_done", p)
                for j in range(half * NJ // 2, (half + 1) * NJ // 2):
                    if j % 2 == 0:
                        done(act, "up_mm", p, j // 2 + 1)
                    nc.scalar.activation(hid[:, j, :], ring[(j // 2) % 2][:, (j % 2) * T * S:(j % 2 + 1) * T * S],
                                         ACT.Relu, scale=ups_man[:, j:j + 1]).then_inc(sems["hid_done"], 1)

            def step(i):
                if active(i - 1):
                    to_rows(i - 1)
                    exps(i - 1, 0)
                if active(i - 2):
                    reciprocal_guess(i - 2)
                if active(i - 1):
                    exps(i - 1, 1)
                    done(act, "attT_tr", i - 1)
                    freed(act, "wo_mm", i - 1)
                    nc.scalar.activation(attT_sb[:].rearrange("p c t s -> p (c t s)"), bank[4][:], ACT.Copy)\
                        .then_inc(sems["attT_out"], 1)
                if active(i):
                    done(act, "qkv_out", i, 1)
                    freed(act, "ssum_done", i)
                    nc.scalar.activation(sq[:], qk[:], ACT.Square).then_inc(sems["sq_done"], 1)
                if active(i - 3):
                    relu(i - 3, 0)
                if active(i):
                    done(act, "qn_done", i)
                    nc.scalar.activation(stack[:, :, :, 0, :].rearrange("p t h d -> p (t h) d"), qn[:], ACT.Copy)\
                        .then_inc(sems["hi_done"], 1)
                if active(i - 3):
                    relu(i - 3, 1)
                if active(i - 1):
                    done(act, "x1T_tr", i - 1)
                    freed(act, "ratio_done", i - 1)
                    for c in range(NC):
                        nc.scalar.activation(ke[:, 1, c], bank[5][:, c * T * S:(c + 1) * T * S]
                                             .rearrange("p (t s) -> p t s", t=T), ACT.Exp, bias=ln_max[:, 0:1])\
                            .then_inc(sems["ek_done"], 1)
                if active(i - 2):
                    done(act, "x2T_tr", i - 2)
                    freed(act, "up_mm", i - 2)
                    nc.scalar.activation(x2hi[:].rearrange("p c t s -> p (c t s)"), bank[4][:], ACT.Copy)\
                        .then_inc(sems["x2hi_done"], 1)

            pipeline(act, step)

        @block.gpsimd
        def _(pool):
            nc.gpsimd.memset(half_neg[:], -0.5).then_inc(consts_done, 1)
            nc.gpsimd.memset(ln_max[:], -LN_MAX).then_inc(consts_done, 1)
            nc.gpsimd.memset(v_sb[:], 1.0).then_inc(consts_done, 1)
            pool.wait_ge(params_in, PARAMS)
            nc.gpsimd.tensor_copy(id_h[:], id_f[:]).then_inc(consts_done, 1)
            nc.gpsimd.tensor_copy(id_b[:], id_f[:]).then_inc(consts_done, 1)
            nc.gpsimd.tensor_copy(mask_bf[:], mask_f[:].unsqueeze(1).to_broadcast([128, REP, 128]))\
                .then_inc(consts_done, 1)
            pool.wait_ge(consts_done, 6)
            pool.wait_ge(setup_act, 4)
            pool.wait_ge(setup_dve, 12)

            def inverse_root(n, p):
                done(pool, f"ag{n + 1}", p)
                alone(pool)
                nc.gpsimd.tensor_scalar(veps[n][:], mv[n][:, :, 1], LN_EPS, 1.0, ALU.add, ALU.mult)\
                    .then_inc(sems[f"ve{n + 1}"], 1)
                done(pool, f"ve{n + 1}", p)
                nc.gpsimd.tensor_tensor(rstd[n][:], veps[n][:], half_neg[:, 0:T], ALU.pow)\
                    .then_inc(sems[f"rs{n + 1}"], 1)

            def rope_products(p):
                done(pool, "qkv_out", p, 1)
                freed(pool, "rot_done", p)
                half = HD // 2
                c = cos_sb[:].unsqueeze(1).to_broadcast([128, T * NQK, HD])
                nc.gpsimd.tensor_tensor(rope_a[:], qk[:], c, ALU.mult).then_inc(sems["rope_done"], 1)
                for to, of in ((0, half), (half, 0)):
                    s = sin_sb[:, to:to + half].unsqueeze(1).to_broadcast([128, T * NQK, half])
                    nc.gpsimd.tensor_tensor(rope_b[:, :, to:to + half], qk[:, :, of:of + half], s, ALU.mult)\
                        .then_inc(sems["rope_done"], 1)

            def rms_scale(p):
                done(pool, "ssum_done", p)
                alone(pool)
                nc.gpsimd.tensor_scalar(msq[:], ssum[:], 1.0 / HD, RMS_EPS, ALU.mult, ALU.add)\
                    .then_inc(sems["msq_done"], 1)
                done(pool, "msq_done", p)
                nc.gpsimd.tensor_tensor(rinv[:], msq[:], half_neg[:], ALU.pow).then_inc(sems["rinv_done"], 1)
                done(pool, "rinv_done", p)
                freed(pool, "qn_done", p)
                nc.gpsimd.tensor_tensor(rscale[:], rinv[:], gain_b[:].rearrange("p t h -> p (t h)"), ALU.mult)\
                    .then_inc(sems["rscale_done"], 1)

            def fill_stack(p):
                done(pool, "hi_done", p)
                done(pool, "lo_done", p)
                alone(pool)
                nc.gpsimd.tensor_copy(stack[:, :, 0:H, 2:4, :].rearrange("p t h r d -> p t h (r d)"),
                                      stack[:, :, 0:H, 0:2, :].rearrange("p t h r d -> p t h (r d)"))\
                    .then_inc(sems["stack_done"], 1)
                for to, of in ((2, 1), (3, 0)):
                    alone(pool)
                    nc.gpsimd.tensor_copy(stack[:, :, H:NQK, to, :], stack[:, :, H:NQK, of, :])\
                        .then_inc(sems["stack_done"], 1)

            def step(i):
                if active(i - 2):
                    done(pool, "rec0_done", i - 2)
                    nc.gpsimd.tensor_tensor(newt[:], ratio[:, 1], rec0[:], ALU.mult).then_inc(sems["newt_done"], 1)
                    done(pool, "nrec_done", i - 2)
                    nc.gpsimd.tensor_tensor(ny[:], ratio[:, 0], nrec[:], ALU.mult).then_inc(sems["ny_done"], 1)
                if active(i - 1):
                    done(pool, "x_in", i - 1)
                    freed(pool, "r1_done", i - 1)
                    nc.gpsimd.tensor_tensor(xb_sb[:], x_sb[:], bo_b[:].unsqueeze(1).to_broadcast([128, T, D]), ALU.add)\
                        .then_inc(sems["xb_done"], 1)
                if active(i):
                    rope_products(i)
                if active(i - 1):
                    inverse_root(0, i - 1)
                if active(i):
                    rms_scale(i)
                if active(i - 2):
                    inverse_root(1, i - 2)
                if active(i - 3):
                    freed(pool, "dn_mm", i - 3)
                    for n in range(NJ // 2):
                        done(pool, "hid_done", i - 3, 2 * n + 2)
                        alone(pool)
                        nc.gpsimd.tensor_copy(hid_hi[:, 2 * n:2 * n + 2], hid[:, 2 * n:2 * n + 2])\
                            .then_inc(sems["hidhi_done"], 1)
                if active(i):
                    fill_stack(i)
                if active(i - 1):
                    p = i - 1
                    done(pool, "ctx_in", p)
                    done(pool, "ek_done", p)
                    nc.gpsimd.tensor_tensor(ke[:, 0], ke[:, 1], ctxT_sb[:], ALU.mult).then_inc(sems["kv_done"], 1)
                    done(pool, "kv_done", p)
                    freed(pool, "ratio_done", p)
                    for c in range(NC):
                        alone(pool)
                        nc.gpsimd.tensor_scalar(now[:, :, c].rearrange("p a t s -> p a (t s)"),
                                                ke[:, :, c].rearrange("p a t s -> p a (t s)"),
                                                e_now[:, c:c + 1], 1.0, ALU.mult, ALU.mult).then_inc(sems["now_done"], 1)
                if active(i - 3):
                    done(pool, "o3_done", i - 3)
                    nc.gpsimd.tensor_tensor(r3[:], o3[:], x2_keep[:], ALU.add).then_inc(sems["r3_done"], 1)
                if active(i - 2):
                    done(pool, "x2_done", i - 2)
                    if active(i - 3):
                        done(pool, "r3_done", i - 3)
                    alone(pool)
                    nc.gpsimd.tensor_copy(x2_keep[:], x2[:]).then_inc(sems["kept"], 1)
                if active(i - 3):
                    inverse_root(2, i - 3)

            pipeline(pool, step)

        @block.vector
        def _(dve):
            dve.wait_ge(params_in, PARAMS)
            nc.vector.tensor_scalar(u_pos[:], tfirst[:], 0.0, None, ALU.max).then_inc(setup_dve, 1)
            nc.vector.tensor_scalar(u_neg[:], tfirst[:], 0.0, None, ALU.min).then_inc(setup_dve, 1)
            nc.vector.memset(dec_sb[:], 1.0).then_inc(setup_dve, 1)
            nc.vector.memset(state[:], 0.0).then_inc(setup_dve, 1)
            nc.vector.tensor_scalar(ups_pow[:].bitcast(I32), ups_sb[:].bitcast(I32), 0x7F800000, None, ALU.bitwise_and)\
                .then_inc(setup_dve, 1)
            nc.vector.tensor_scalar(ups_man[:].bitcast(I32), ups_sb[:].bitcast(I32), -0x7F800001, 0x3F800000,
                                    ALU.bitwise_and, ALU.bitwise_or).then_inc(setup_dve, 1)
            nc.vector.tensor_scalar(dsc_b[:], dsc_b[:], osc_b[:, 0:1], None, ALU.mult).then_inc(setup_dve, 1)
            nc.vector.memset(gain_b[:], 1.0).then_inc(setup_dve, 1)
            dve.wait_ge(setup_dve, 8)
            nc.vector.tensor_scalar(gain_b[:, :, 0:H], gain_in[:], HD ** -0.5, None, ALU.mult).then_inc(setup_dve, 1)
            dve.wait_ge(setup_act, 2)
            dve.wait_ge(setup_dve, 9)
            for c in range(NC):
                nc.vector.tensor_scalar(dec_sb[:, :, c].rearrange("p a t s -> p a (t s)"),
                                        dec_sb[:, :, c].rearrange("p a t s -> p a (t s)"),
                                        tdec[:, c:c + 1], None, ALU.mult).then_inc(setup_dve, 1)
            dve.wait_ge(setup_dve, 11)
            nc.vector.memset(dec_sb[:].rearrange("p a c t s -> p (a c t) s")[:, :, 0:1], 0.0).then_inc(setup_dve, 1)
            dve.wait_ge(setup_act, 5)
            for j in range(NJ):
                nc.vector.tensor_scalar(dn_sb[:, j], dn_f[:, j], ups_pow[:, j:j + 1], None, ALU.mult).then_inc(signs_done, 1)
            dve.wait_ge(setup_dve, 12)
            dve.wait_ge(consts_done, 6)

            def attend_norm(p, t):
                done(dve, "pv_mm", p, 4 * (t + 1))
                o = bank[4 - 2 * t][:, 0:H * (HD + 1)].rearrange("p (h d) -> p h d", h=H)
                nc.vector.reciprocal(prec[:, t, :].unsqueeze(2), o[:, :, HD:HD + 1]).then_inc(sems["prec_done"], 1)
                done(dve, "prec_done", p, t + 1)
                freed(dve, "attT_tr", p)
                nc.vector.tensor_tensor(att[:, t], o[:, :, 0:HD], prec[:, t].unsqueeze(2).to_broadcast([128, H, HD]),
                                        ALU.mult).then_inc(sems["att_done"], 1)

            def moments(n, p, rows):
                for t in range(T):
                    nc.vector.bn_stats(stats[n][:, t], rows[:, t, :]).then_inc(sems[f"bn{n + 1}"], 1)
                for t in range(T):
                    done(dve, f"bn{n + 1}", p, t + 1)
                    alone(dve)
                    nc.vector.bn_aggr(mv[n][:, t], stats[n][:, t]).then_inc(sems[f"ag{n + 1}"], 1)

            def normed(n, p, rows, to, name):
                done(dve, f"rs{n + 1}", p)
                for t in range(T):
                    nc.vector.tensor_scalar(to[:, t], rows[:, t, :], mv[n][:, t, 0:1], rstd[n][:, t:t + 1],
                                            ALU.subtract, ALU.mult).then_inc(sems[name], 1)

            W = NC * T * S

            def scan(p):
                done(dve, "now_done", p)
                nc.vector.tensor_tensor_scan(state[:, 1:2 * W + 1], dec_sb[:].rearrange("p a c t s -> p (a c t s)"),
                                             ke[:].rearrange("p a c t s -> p (a c t s)"), 0.0, ALU.mult, ALU.add)\
                    .then_inc(sems["scan_done"], 1)
                done(dve, "scan_done", p)
                nc.vector.tensor_copy(state[:, 0:2 * W].rearrange("p (n s) -> p n s", s=S)[:, :, 0:1],
                                      ke[:].rearrange("p a c t s -> p (a c t) s")[:, :, 0:1]).then_inc(sems["fix_done"], 1)
                done(dve, "fix_done", p)
                for c in range(NC):
                    nc.vector.scalar_tensor_tensor(
                        ratio[:, :, c].rearrange("p a t s -> p a (t s)"),
                        state[:, 0:2 * W].rearrange("p (a c n) -> p a c n", a=2, c=NC)[:, :, c, :],
                        e_state[:, c:c + 1], now[:, :, c].rearrange("p a t s -> p a (t s)"),
                        ALU.mult, ALU.add).then_inc(sems["ratio_done"], 1)

            def step(i):
                if active(i - 1):
                    p = i - 1
                    done(dve, "qT_tr", p)
                    freed(dve, "scores_mm", p)
                    nc.vector.tensor_copy(qT_sb[:, 1].rearrange("p b s -> p (b s)"), bank[3].bitcast(F16)[:])\
                        .then_inc(sems["q1_out"], 1)
                if active(i - 2):
                    scan(i - 2)
                if active(i - 1):
                    attend_norm(i - 1, 0)
                if active(i - 2):
                    p = i - 2
                    done(dve, "newt_done", p)
                    nc.vector.scalar_tensor_tensor(nrec[:], newt[:], 2.0, rec0[:], ALU.subtract, ALU.mult)\
                        .then_inc(sems["nrec_done"], 1)
                    done(dve, "ny_done", p)
                    freed(dve, "zT_tr", p)
                    nc.vector.tensor_tensor(zT[:].rearrange("p c t s -> p (c t s)"), bank[5][:],
                                            ny[:].rearrange("p c t s -> p (c t s)"), ALU.subtract)\
                        .then_inc(sems["z_done"], 1)
                if active(i - 1):
                    attend_norm(i - 1, 1)
                if active(i):
                    done(dve, "qkv_mm", i)
                    for t in range(T):
                        pass
                    freed(dve, "sq_done", i)
                    freed(dve, "rope_done", i)
                    for t in range(T):
                        q = bank[3 * t]
                        ins = nc.vector.tensor_tensor(qk[:, t * NQK:(t + 1) * NQK, :].rearrange("p h d -> p (h d)"),
                                                      q[:, 0:NQK * HD], bqk_b[:, 0:NQK * HD], ALU.add)
                    ins.then_inc(sems["qkv_out"], 1)
                    for t in range(T):
                        ins = nc.vector.tensor_tensor(v_sb[:, t, :, 0:HD],
                                                      bank[3 * t][:, NQK * HD:E].rearrange("p (g d) -> p g d", g=KVH),
                                                      bqk_b[:, NQK * HD:E].rearrange("p (g d) -> p g d", g=KVH), ALU.add)
                    ins.then_inc(sems["qkv_out"], 1)
                if active(i - 1):
                    p = i - 1
                    done(dve, "wo_mm", p)
                    done(dve, "xb_done", p)
                    nc.vector.tensor_tensor(r1[:].rearrange("p t d -> p (t d)"), bank[2][:],
                                            xb_sb[:].rearrange("p t d -> p (t d)"), ALU.add).then_inc(sems["r1_done"], 1)
                    done(dve, "r1_done", p)
                    moments(0, p, r1)
                if active(i):
                    done(dve, "sq_done", i)
                    nc.vector.tensor_reduce(ssum[:], sq[:], AX_X, ALU.add).then_inc(sems["ssum_done"], 1)
                if active(i - 1):
                    freed(dve, "x1T_tr", i - 1)
                    normed(0, i - 1, r1, x1, "x1_done")
                if active(i):
                    done(dve, "rope_done", i)
                    nc.vector.tensor_tensor(rot[:], rope_a[:], rope_b[:], ALU.add).then_inc(sems["rot_done"], 1)
                    done(dve, "rot_done", i)
                    done(dve, "rscale_done", i)
                    nc.vector.tensor_tensor(qn[:], rot[:], rscale[:].unsqueeze(2).to_broadcast([128, T * NQK, HD]),
                                            ALU.mult).then_inc(sems["qn_done"], 1)
                if active(i - 2):
                    p = i - 2
                    z = bank[0][:].rearrange("p (t d) -> p t d", t=T)
                    done(dve, "zT_tr", p)
                    moments(1, p, z)
                if active(i):
                    done(dve, "hi_done", i)
                    nc.vector.tensor_tensor(stack[:, :, :, 1, :].rearrange("p t h d -> p (t h) d"), qn[:],
                                            stack[:, :, :, 0, :].rearrange("p t h d -> p (t h) d"), ALU.subtract)\
                        .then_inc(sems["lo_done"], 1)
                if active(i - 2):
                    freed(dve, "x2T_tr", p)
                    freed(dve, "kept", p)
                    normed(1, p, z, x2, "x2_done")
                if active(i - 3):
                    for n in range(NJ // 2):
                        done(dve, "hidhi_done", i - 3, n + 1)
                        nc.vector.tensor_tensor(hid_lo[:, 2 * n:2 * n + 2], hid[:, 2 * n:2 * n + 2],
                                                hid_hi[:, 2 * n:2 * n + 2], ALU.subtract).then_inc(sems["hidlo_done"], 1)
                if active(i - 2):
                    done(dve, "x2hi_done", i - 2)
                    nc.vector.tensor_tensor(x2lo[:].rearrange("p c t s -> p (c t s)"), bank[4][:],
                                            x2hi[:].rearrange("p c t s -> p (c t s)"), ALU.subtract)\
                        .then_inc(sems["x2lo_done"], 1)
                if active(i - 3):
                    p = i - 3
                    done(dve, "dn_mm", p)
                    freed(dve, "r3_done", p)
                    nc.vector.tensor_tensor(o3[:], bank[1][:].rearrange("p (t d) -> p t d", t=T),
                                            dsc_b[:].unsqueeze(1).to_broadcast([128, T, D]), ALU.mult)\
                        .then_inc(sems["o3_done"], 1)
                    done(dve, "r3_done", p)
                    moments(2, p, r3)
                    freed(dve, "stored", p)
                    normed(2, p, r3, outb, "out_done")

            pipeline(dve, step)


def kernel(x, ctx_2048, L0_attn_Wq, L0_attn_bq, L0_attn_Wk, L0_attn_bk, L0_attn_Wv, L0_attn_bv, L0_attn_Wo,
           L0_attn_bo, L0_attn_q_gain, L0_xattn_time_decay, L0_xattn_time_first, L0_ffn_up_weight,
           L0_ffn_down_weight, L0_ffn_up_scale, L0_ffn_down_scale, L0_ffn_output_scale):
    import concourse.bacc as bacc
    from concourse.bass_utils import run_bass_kernel_spmd

    def a(v):
        return np.asarray(v)

    order = np.arange(H).reshape(2, 2, REP).transpose(0, 2, 1).reshape(H)
    wq = a(L0_attn_Wq).reshape(H, HD, D)[order].reshape(D, D)
    bq = a(L0_attn_bq).reshape(H, HD)[order].reshape(D)

    def chunked(w):
        return np.ascontiguousarray(w.reshape(-1, 128, w.shape[1]).transpose(1, 0, 2))

    def to_channels(v):
        return np.ascontiguousarray(a(v).reshape(PAIRS, T, S, NC, 128).transpose(0, 4, 3, 1, 2))

    inv_freq = (np.float32(1.0) / np.float32(10000.0) ** (np.arange(0, HD, 2, dtype=np.float32) / np.float32(HD)))
    freqs = np.outer(np.arange(S, dtype=np.float32), inv_freq.astype(np.float32)).astype(np.float32)
    cos, sin = np.cos(freqs), np.sin(freqs)
    key, query = np.arange(S)[:, None], np.arange(S)[None, :]
    scale = np.ones(1, np.float32)

    arrays = {
        "x": np.ascontiguousarray(a(x).reshape(PAIRS, T, S, D).transpose(0, 2, 1, 3)),
        "xT": to_channels(x),
        "ctxT": to_channels(ctx_2048),
        "wqkv": chunked(np.concatenate([wq, a(L0_attn_Wk), a(L0_attn_Wv)]).T),
        "bqkv": np.concatenate([bq, a(L0_attn_bk), a(L0_attn_bv)]),
        "gains": a(L0_attn_q_gain)[order],
        "wo": chunked(a(L0_attn_Wo).T),
        "bo": a(L0_attn_bo),
        "decay_in": np.ascontiguousarray(a(L0_xattn_time_decay).reshape(NC, 128).T),
        "first_in": np.ascontiguousarray(a(L0_xattn_time_first).reshape(NC, 128).T),
        "up": chunked(a(L0_ffn_up_weight).T),
        "down": chunked(a(L0_ffn_down_weight).T),
        "up_s": np.ascontiguousarray(a(L0_ffn_up_scale).reshape(NJ, 128).T),
        "down_s": a(L0_ffn_down_scale),
        "out_s": a(L0_ffn_output_scale),
        "rope_cos": np.concatenate([cos, cos], 1).astype(np.float32),
        "rope_sin": np.concatenate([sin, -sin], 1).astype(np.float32),
        "mask_in": np.where(key > query, np.float32(MASKED), np.float32(0.0)).astype(np.float32),
        "ident_in": np.eye(128, dtype=np.float32),
    }
    nc = bacc.Bacc("TRN2", target_bir_lowering=False, num_devices=1)
    args = [nc.dram_tensor(f"{n}_dram", v.shape, F32, kind="ExternalInput").ap() for n, v in arrays.items()]
    result = nc.dram_tensor("out_dram", (PAIRS, S, T, D), F32, kind="ExternalOutput").ap()
    build(nc, *args, result)
    r = run_bass_kernel_spmd(nc, [{f"{n}_dram": v for n, v in arrays.items()}], core_ids=[0])
    got = r.results[0]["out_dram"]
    return np.ascontiguousarray(got.reshape(PAIRS, S, T, D).transpose(0, 2, 1, 3)).reshape(B, S, D)
```

```python
from contextlib import ExitStack

import numpy as np

import concourse.bass as bass
from concourse import mybir

ALU = mybir.AluOpType
ACT = mybir.ActivationFunctionType
F32 = mybir.dt.float32
F16 = mybir.dt.float16
BF16 = mybir.dt.bfloat16
I32 = mybir.dt.int32
AX_X = mybir.AxisListType.X

B, S, D = 16, 128, 256
H, KVH = 16, 4
HD = D // H
KVD = KVH * HD
NQK = H + KVH
DFF = 1024
T = 2
PAIRS = B // T
NC = D // 128
NJ = DFF // 128
E = D + 2 * KVD
REP = H // KVH
VW = 32
MASKED = -1e30
BLOCKS = NQK // 2
QBLOCKS = H // 2
RMS_EPS = 1.1920929e-07
LN_EPS = 1e-5
LN_MAX = float(D) ** 0.5
DEPTH = 3
PEELED = DEPTH + 1


def first(p):
    return isinstance(p, int) and p == 0


def active(p):
    return not isinstance(p, int) or 0 <= p < PAIRS


def build(nc, x, xT, ctxT, wqkv, bqkv, gains, wo, bo, decay_in, first_in, up, down, up_s, down_s, out_s,
          rope_cos, rope_sin, ident_in, out):
    with ExitStack() as ctx:
        def sb(name, shape, dt=F32):
            return ctx.enter_context(nc.sbuf_tensor(name, shape, dt))

        def sem(name):
            return ctx.enter_context(nc.semaphore(name))

        bank = [ctx.enter_context(nc.psum_tensor(f"bank{n}", [128, 512], F32)) for n in range(8)]
        ring = [bank[6], bank[7]]

        wqkv_sb = sb("wqkv_sb", [128, NC, E])
        wo_sb = sb("wo_sb", [128, NC, D])
        bqk_b = sb("bqk_b", [128, E])
        gain_in = sb("gain_in", [128, T, H])
        gain_b = sb("gain_b", [128, T, NQK])
        bo_b = sb("bo_b", [128, D])
        dsc_b = sb("dsc_b", [128, D])
        osc_b = sb("osc_b", [128, 1])
        cos_sb = sb("cos_sb", [128, HD])
        sin_sb = sb("sin_sb", [128, HD])
        id_f = sb("id_f", [128, 128])
        id_h = sb("id_h", [128, 128], F16)
        id_b = sb("id_b", [128, 128], BF16)
        mask_f = sb("mask_f", [128, REP, S])
        mask_sb = sb("mask_sb", [128, REP, S], BF16)
        up_f = sb("up_f", [128, NC, DFF])
        up_sb = sb("up_sb", [128, NC, DFF], F16)
        dn_f = sb("dn_f", [128, NJ, D])
        dn_sb = sb("dn_sb", [128, NJ, D], BF16)
        ups_sb = sb("ups_sb", [128, NJ])
        ups_pow = sb("ups_pow", [128, NJ])
        ups_man = sb("ups_man", [128, NJ])
        tdec = sb("tdec", [128, NC])
        tdec2 = sb("tdec2", [128, NC])
        tfirst = sb("tfirst", [128, NC])
        e_state = sb("e_state", [128, NC])
        e_now = sb("e_now", [128, NC])
        u_neg = sb("u_neg", [128, NC])
        u_pos = sb("u_pos", [128, NC])
        dec_sb = sb("dec_sb", [128, 2, NC, T, S])
        half_neg = sb("half_neg", [128, T * NQK])
        ln_max = sb("ln_max", [128, 1])

        xT_sb = sb("xT_sb", [128, NC, T, S])
        x_sb = sb("x_sb", [128, T, D])
        ctxT_sb = sb("ctxT_sb", [128, NC, T, S])
        xb_sb = sb("xb_sb", [128, T, D])
        qk = sb("qk", [128, T * NQK, HD])
        v_sb = sb("v_sb", [128, T, KVH, VW])
        sq = sb("sq", [128, T * NQK, HD])
        ssum = sb("ssum", [128, T * NQK])
        msq = sb("msq", [128, T * NQK])
        lnms = sb("lnms", [128, T * NQK])
        y0 = sb("y0", [128, T * NQK])
        ysq = sb("ysq", [128, T * NQK])
        vy = sb("vy", [128, T * NQK])
        ny0 = sb("ny0", [128, T * NQK])
        rscale = sb("rscale", [128, T * NQK])
        rope_a = sb("rope_a", [128, T * NQK, HD])
        rope_b = sb("rope_b", [128, T * NQK, HD])
        rot = sb("rot", [128, T * NQK, HD])
        qn = sb("qn", [128, T * NQK, HD])
        stack = sb("stack", [128, T, NQK, 4, HD], F16)
        qT_sb = sb("qT_sb", [128, T, QBLOCKS, 128], F16)
        kT_sb = sb("kT_sb", [128, T, 2, 128], F16)
        probs = sb("probs", [128, KVH, REP, 128])
        prec = sb("prec", [128, T, H])
        att_un = sb("att_un", [128, T, REP, S])
        att = sb("att", [128, T, H, HD])
        attT_sb = sb("attT_sb", [128, NC, T, 128])
        r1 = sb("r1", [128, T, D])
        x1 = sb("x1", [128, T, D])
        stats = [sb(f"stats{n}", [128, T, 6]) for n in range(3)]
        mv = [sb(f"mv{n}", [128, T, 2]) for n in range(3)]
        veps = [sb(f"veps{n}", [128, T]) for n in range(3)]
        rstd = [sb(f"rstd{n}", [128, T]) for n in range(3)]
        ke = sb("ke", [128, 2, NC, T, S])
        state = sb("state", [128, 2 * NC * T * S + 2])
        now = sb("now", [128, 2, NC, T, S])
        ratio = sb("ratio", [128, 2, NC, T, S])
        lnden = sb("lnden", [128, NC, T, S])
        rec0 = sb("rec0", [128, NC, T, S])
        newt = sb("newt", [128, NC, T, S])
        nrec = sb("nrec", [128, NC, T, S])
        ny = sb("ny", [128, NC, T, S])
        zT = sb("zT", [128, NC, T, S])
        x2 = sb("x2", [128, T, D])
        x2_keep = sb("x2_keep", [128, T, D])
        x2hi = sb("x2hi", [128, NC, T, S], F16)
        x2lo = sb("x2lo", [128, NC, T, S], F16)
        hid = sb("hid", [128, NJ, T * S])
        hid_hi = sb("hid_hi", [128, NJ, T * S], F16)
        hid_lo = sb("hid_lo", [128, NJ, T * S], F16)
        o3 = sb("o3", [128, T, D])
        r3 = sb("r3", [128, T, D])
        outb = sb("outb", [128, T, D])

        names = dict(
            xT_in=16, x_in=16, ctx_in=16, stored=16,
            qkv_mm=2, kT_tr=1, qT_tr=2, scores_mm=8, pv_mm=8, attT_tr=1, wo_mm=1, x1T_tr=1, zT_tr=1,
            x2T_tr=1, un_out=2, un_tr=2, up_mm=4, dn_mm=1,
            qk_out=1, v_out=1, sq_done=1, ssum_done=1, msq_done=1, rinv_done=1, rscale_done=1, rope_done=3, ln_rms=1, y0_done=1, ysq_done=1, vy_done=1, ny0_done=1,
            rot_done=1, qn_done=1, hi_done=1, lo_done=1, stack_done=3, kT_out=1, q0_out=1, q1_out=1,
            probs_done=8, prec_done=2, att_done=2, attT_out=1, xb_done=1, r1_done=1, bn1=2, ag1=2, ve1=1,
            rs1=1, x1_done=2, ek_done=2, kv_done=1, now_done=2, scan_done=1, fix_done=1, ratio_done=2,
            ln_done=1, rec0_done=1, newt_done=1, nrec_done=1, ny_done=1, z_done=1, bn2=2, ag2=2, ve2=1,
            rs2=1, x2_done=2, kept=16, x2hi_done=1, x2lo_done=1, hid_done=8, hidhi_done=4, hidlo_done=4,
            o3_done=1, r3_done=1, bn3=2, ag3=2, ve3=1, rs3=1, out_done=2)
        sems = {n: sem(n) for n in names}
        params_in = sem("params_in")
        ffn_in = sem("ffn_in")
        signs_done = sem("signs_done")
        consts_done = sem("consts_done")
        setup_dve = sem("setup_dve")
        setup_act = sem("setup_act")

        def done(eng, name, p, k=None):
            eng.wait_ge(sems[name], p * names[name] + (names[name] if k is None else k))

        def freed(eng, name, p, back=1, k=None):
            if not (isinstance(p, int) and p < back):
                done(eng, name, p - back, k)

        def alone(eng):
            eng.nop(nofuse=True)

        consts = [(wqkv_sb[:], wqkv), (id_f[:], ident_in), (wo_sb[:], wo),
                  (cos_sb[:], rope_cos), (sin_sb[:], rope_sin),
                  (bqk_b[:], bqkv.partition_broadcast(128)), (bo_b[:], bo.partition_broadcast(128)),
                  (gain_in[:, 0, :], gains.partition_broadcast(128)), (gain_in[:, 1, :], gains.partition_broadcast(128)),
                  (dsc_b[:], down_s.partition_broadcast(128)), (osc_b[:], out_s.partition_broadcast(128)),
                  (tdec[:], decay_in), (tfirst[:], first_in), (ups_sb[:], up_s)]
        PARAMS = 16 * len(consts)

        block = ctx.enter_context(nc.Block())

        def pipeline(eng, step, last_extra=0):
            for i in range(PEELED):
                step(i)
            with eng.Fori(PEELED, PAIRS) as i:
                step(i)
            for i in range(PAIRS, PAIRS + DEPTH):
                step(i)

        @block.sync
        def _(sp):
            sp.dma_start(xT_sb[:], xT[0]).then_inc(sems["xT_in"], 16)
            for dst, src in consts:
                sp.dma_start(dst, src).then_inc(params_in, 16)
            sp.dma_start(x_sb[:], x[0]).then_inc(sems["x_in"], 16)
            sp.dma_start(ctxT_sb[:], ctxT[0]).then_inc(sems["ctx_in"], 16)
            sp.dma_start(up_f[:], up).then_inc(ffn_in, 16)
            sp.dma_start(dn_f[:], down).then_inc(ffn_in, 16)

            def step(i):
                if not isinstance(i, int) or i + 1 < PAIRS:
                    done(sp, "qkv_mm", i)
                    sp.dma_start(xT_sb[:], xT[i + 1]).then_inc(sems["xT_in"], 16)
                if not isinstance(i, int) or 1 <= i < PAIRS:
                    done(sp, "xb_done", i - 1)
                    sp.dma_start(x_sb[:], x[i]).then_inc(sems["x_in"], 16)
                    done(sp, "kv_done", i - 1)
                    sp.dma_start(ctxT_sb[:], ctxT[i]).then_inc(sems["ctx_in"], 16)
                if active(i - 2):
                    done(sp, "x2_done", i - 2)
                    freed(sp, "r3_done", i - 2)
                    sp.dma_start(x2_keep[:], x2[:]).then_inc(sems["kept"], 16)
                if active(i - 3):
                    done(sp, "out_done", i - 3)
                    sp.dma_start(out[i - 3], outb[:]).then_inc(sems["stored"], 16)

            for i in range(PEELED):
                step(i)
            with sp.Fori(PEELED, PAIRS - 1) as i:
                step(i)
            for i in range(PAIRS - 1, PAIRS + DEPTH):
                step(i)
            sp.wait_ge(sems["stored"], 16 * PAIRS)

        @block.tensor
        def _(pe):
            pe.wait_ge(params_in, PARAMS)
            pe.wait_ge(consts_done, 8)

            def heads_to_rows(p):
                done(pe, "stack_done", p)
                freed(pe, "r1_done", p)
                for t in range(T):
                    for b in range(2):
                        mm = nc.tensor.transpose(bank[2].bitcast(F16)[:, (2 * t + b) * 128:(2 * t + b + 1) * 128],
                                                 stack[:, t, H + 2 * b:H + 2 * b + 2, :, :].rearrange("p h r d -> p (h r d)"),
                                                 id_h[:])
                mm.then_inc(sems["kT_tr"], 1)
                freed(pe, "x2_done", p, 2)
                for t in range(T):
                    for b in range(QBLOCKS):
                        mm = nc.tensor.transpose(bank[3 * t].bitcast(F16)[:, b * 128:(b + 1) * 128],
                                                 stack[:, t, 2 * b:2 * b + 2, :, :].rearrange("p h r d -> p (h r d)"),
                                                 id_h[:])
                    mm.then_inc(sems["qT_tr"], 1)

            def attend(p, t):
                for g in range(KVH + 2):
                    if g < KVH:
                        n = t * KVH + g
                        if n == 0:
                            done(pe, "kT_out", p)
                        if g == 0:
                            done(pe, f"q{t}_out", p)
                        if g >= 2:
                            done(pe, "probs_done", p, n - 1)
                        elif t == 0:
                            freed(pe, "hid_done", p, 3, k=6 + 2 * g)
                        elif active(p - 2):
                            done(pe, "hid_done", p - 2, 2 + 2 * g)
                        else:
                            done(pe, "probs_done", p, n - 1)
                        r = 64 * (g % 2)
                        nc.tensor.matmul(ring[n % 2][:], kT_sb[r:r + 64, t, g // 2, :],
                                         qT_sb[r:r + 64, t, 4 * (g // 2):4 * (g // 2) + 4, :].rearrange("p a b -> p (a b)"),
                                         start=True, stop=False)
                        nc.tensor.matmul(ring[n % 2][:], id_b[:], mask_sb[:].rearrange("p j s -> p (j s)"),
                                         start=False, stop=True).then_inc(sems["scores_mm"], 1)
                    if g >= 2:
                        n = t * KVH + g - 2
                        if n == 0:
                            freed(pe, "x2lo_done", p, 2)
                        done(pe, "probs_done", p, n + 1)
                        r = VW * (g - 2)
                        nc.tensor.matmul(bank[4 - 2 * t][r:r + VW, :], v_sb[:, t, g - 2, :],
                                         probs[:, g - 2].rearrange("p j s -> p (j s)"),
                                         start=True, stop=True).then_inc(sems["pv_mm"], 1)

            def attention_to_tokens(p, t):
                done(pe, "un_out", p, t + 1)
                for j in range(REP):
                    mm = nc.tensor.transpose(bank[4 - 2 * t][:, j * 128:(j + 1) * 128], att_un[:, t, j, :], id_f[:])
                mm.then_inc(sems["un_tr"], 1)

            def project(p):
                done(pe, "xT_in", p)
                for t in range(T):
                    if not first(p):
                        done(pe, f"q{t}_out", p - 1)
                    for c in range(NC):
                        mm = nc.tensor.matmul(bank[3 * t][:, 0:E], xT_sb[:, c, t, :], wqkv_sb[:, c, :],
                                              start=(c == 0), stop=(c == NC - 1))
                    mm.then_inc(sems["qkv_mm"], 1)

            def attention_to_channels(p):
                done(pe, "att_done", p)
                a = att[:].rearrange("p t h d -> p t (h d)")
                for c in range(NC):
                    for t in range(T):
                        mm = nc.tensor.transpose(bank[4][:, (2 * c + t) * 128:(2 * c + t + 1) * 128],
                                                 a[:, t, c * 128:(c + 1) * 128], id_f[:])
                mm.then_inc(sems["attT_tr"], 1)

            def project_out(p):
                done(pe, "attT_out", p)
                for t in range(T):
                    for c in range(NC):
                        mm = nc.tensor.matmul(bank[2][:, t * D:(t + 1) * D], attT_sb[:, c, t, :], wo_sb[:, c, :],
                                              start=(c == 0), stop=(c == NC - 1))
                mm.then_inc(sems["wo_mm"], 1)

            def mixed_to_tokens(p, i):
                done(pe, "z_done", p)
                if active(i):
                    done(pe, "v_out", i)
                elif active(i - 1):
                    done(pe, "q0_out", i - 1)
                for t in range(T):
                    for c in range(NC):
                        mm = nc.tensor.transpose(bank[0][:, t * D + c * 128:t * D + (c + 1) * 128], zT[:, c, t, :], id_f[:])
                mm.then_inc(sems["zT_tr"], 1)

            def ffn_up(p, i, t):
                if t == 0:
                    done(pe, "x2hi_done", p)
                    done(pe, "x2lo_done", p)
                for n in range(2 * t, 2 * t + 2):
                    if active(i - 1):
                        done(pe, "probs_done", i - 1, KVH * t + 3 + n % 2)
                    elif n >= 2:
                        done(pe, "hid_done", p, 2 * (n - 1))
                    else:
                        freed(pe, "hid_done", p, k=2 * (n + 3))
                    for s in range(2):
                        j = 2 * n + s
                        m = 0
                        for c in range(NC):
                            for part in (x2hi, x2lo):
                                mm = nc.tensor.matmul(ring[n % 2][:, s * T * S:(s + 1) * T * S],
                                                      up_sb[:, c, j * 128:(j + 1) * 128],
                                                      part[:, c, :, :].rearrange("p t s -> p (t s)"),
                                                      start=(m == 0), stop=(m == 2 * NC - 1))
                                m += 1
                    mm.then_inc(sems["up_mm"], 1)

            def x1_to_channels(p):
                done(pe, "x1_done", p)
                freed(pe, "z_done", p)
                for c in range(NC):
                    for t in range(T):
                        mm = nc.tensor.transpose(bank[5][:, (2 * c + t) * 128:(2 * c + t + 1) * 128],
                                                 x1[:, t, c * 128:(c + 1) * 128], id_f[:])
                mm.then_inc(sems["x1T_tr"], 1)

            def x2_to_channels(p, i):
                done(pe, "x2_done", p)
                if active(i - 1):
                    done(pe, "attT_out", i - 1)
                else:
                    freed(pe, "x2lo_done", p)
                for c in range(NC):
                    for t in range(T):
                        mm = nc.tensor.transpose(bank[4][:, (2 * c + t) * 128:(2 * c + t + 1) * 128],
                                                 x2[:, t, c * 128:(c + 1) * 128], id_f[:])
                mm.then_inc(sems["x2T_tr"], 1)

            def ffn_down(p):
                freed(pe, "o3_done", p)
                for t in range(T):
                    for j in range(NJ):
                        if t == 0 and j % 2 == 0:
                            done(pe, "hidhi_done", p, j // 2 + 1)
                            done(pe, "hidlo_done", p, j // 2 + 1)
                        for m, part in enumerate((hid_hi, hid_lo)):
                            mm = nc.tensor.matmul(bank[1][:, t * D:(t + 1) * D], part[:, j, t * S:(t + 1) * S],
                                                  dn_sb[:, j, :], start=(j == 0 and m == 0),
                                                  stop=(j == NJ - 1 and m == 1))
                mm.then_inc(sems["dn_mm"], 1)

            def step(i):
                if active(i - 1):
                    heads_to_rows(i - 1)
                    attend(i - 1, 0)
                if active(i - 3):
                    if isinstance(i, int) and i == 3:
                        pe.wait_ge(signs_done, 1 + NJ)
                    ffn_up(i - 3, i, 0)
                if active(i - 1):
                    attention_to_tokens(i - 1, 0)
                if active(i):
                    project(i)
                if active(i - 1):
                    attend(i - 1, 1)
                if active(i - 3):
                    ffn_up(i - 3, i, 1)
                if active(i - 1):
                    attention_to_tokens(i - 1, 1)
                if active(i - 2):
                    mixed_to_tokens(i - 2, i)
                if active(i - 1):
                    attention_to_channels(i - 1)
                if active(i - 1):
                    project_out(i - 1)
                if active(i - 3):
                    ffn_down(i - 3)
                if active(i - 1):
                    x1_to_channels(i - 1)
                if active(i - 2):
                    x2_to_channels(i - 2, i)

            pipeline(pe, step)

        @block.scalar
        def _(act):
            nc.scalar.preload_act_table_set("natural_log_exp_and_others")
            act.wait_ge(params_in, PARAMS)
            nc.scalar.activation(tdec2[:], tdec[:], ACT.Exp).then_inc(setup_act, 1)
            act.wait_ge(setup_act, 1)
            nc.scalar.activation(tdec[:], tdec2[:], ACT.Exp, scale=-1.0).then_inc(setup_act, 1)
            act.wait_ge(setup_dve, 2)
            nc.scalar.activation(e_state[:], u_pos[:], ACT.Exp, scale=-1.0).then_inc(setup_act, 1)
            nc.scalar.activation(e_now[:], u_neg[:], ACT.Exp).then_inc(setup_act, 1)

            def signs():
                act.wait_ge(ffn_in, 32)
                nc.scalar.activation(up_sb[:], up_f[:], ACT.Sign).then_inc(signs_done, 1)
                nc.scalar.activation(dn_f[:], dn_f[:], ACT.Sign).then_inc(setup_act, 1)

            def to_rows(p):
                done(act, "kT_tr", p)
                freed(act, "scores_mm", p)
                nc.scalar.activation(kT_sb[:], bank[2].bitcast(F16)[:, 0:512].rearrange("p (t b s) -> p t b s", t=T, b=2),
                                     ACT.Copy).then_inc(sems["kT_out"], 1)
                done(act, "qT_tr", p, 1)
                nc.scalar.activation(qT_sb[:, 0], bank[0].bitcast(F16)[:].rearrange("p (b s) -> p b s", b=QBLOCKS),
                                     ACT.Copy).then_inc(sems["q0_out"], 1)

            def exps(p, t):
                for g in range(KVH):
                    n = t * KVH + g
                    done(act, "scores_mm", p, n + 1)
                    if n >= KVH:
                        done(act, "pv_mm", p, n - KVH + 1)
                    else:
                        freed(act, "pv_mm", p, k=n + KVH + 1)
                    nc.scalar.activation(probs[:, g].rearrange("p a b -> p (a b)"), ring[n % 2][:], ACT.Exp)\
                        .then_inc(sems["probs_done"], 1)

            def take_products(p, t):
                done(act, "pv_mm", p, KVH * (t + 1))
                freed(act, "un_tr", p, k=t + 1)
                nc.scalar.activation(att_un[:, t].rearrange("p j s -> p (j s)"), bank[4 - 2 * t][:], ACT.Copy)\
                    .then_inc(sems["un_out"], 1)

            def reciprocal_guess(p):
                done(act, "ratio_done", p)
                nc.scalar.activation(lnden[:], ratio[:, 1], ACT.Ln).then_inc(sems["ln_done"], 1)
                done(act, "ln_done", p)
                freed(act, "nrec_done", p)
                nc.scalar.activation(rec0[:], lnden[:], ACT.Exp, scale=-1.0).then_inc(sems["rec0_done"], 1)

            def relu(p, half):
                if half == 0:
                    freed(act, "hidlo_done", p)
                    freed(act, "dn_mm", p)
                for n in range(2 * half, 2 * half + 2):
                    done(act, "up_mm", p, n + 1)
                    for j in (2 * n, 2 * n + 1):
                        nc.scalar.activation(hid[:, j, :], ring[n % 2][:, (j % 2) * T * S:(j % 2 + 1) * T * S],
                                             ACT.Relu, scale=ups_man[:, j:j + 1]).then_inc(sems["hid_done"], 1)
                    done(act, "hid_done", p, 2 * n + 2)
                    nc.scalar.activation(hid_hi[:, 2 * n:2 * n + 2], hid[:, 2 * n:2 * n + 2], ACT.Copy)\
                        .then_inc(sems["hidhi_done"], 1)

            def step(i):
                if active(i - 1):
                    to_rows(i - 1)
                    exps(i - 1, 0)
                    take_products(i - 1, 0)
                if active(i - 2):
                    reciprocal_guess(i - 2)
                if active(i - 3):
                    relu(i - 3, 0)
                if active(i):
                    done(act, "qk_out", i)
                    freed(act, "ssum_done", i)
                    nc.scalar.activation(sq[:], qk[:], ACT.Square).then_inc(sems["sq_done"], 1)
                if active(i - 1):
                    exps(i - 1, 1)
                    take_products(i - 1, 1)
                if active(i):
                    done(act, "msq_done", i)
                    nc.scalar.activation(lnms[:], msq[:], ACT.Ln).then_inc(sems["ln_rms"], 1)
                    done(act, "ln_rms", i)
                    freed(act, "ny0_done", i)
                    nc.scalar.activation(y0[:], lnms[:], ACT.Exp, scale=-0.5).then_inc(sems["y0_done"], 1)
                if active(i - 1):
                    done(act, "attT_tr", i - 1)
                    freed(act, "wo_mm", i - 1)
                    nc.scalar.activation(attT_sb[:].rearrange("p c t s -> p (c t s)"), bank[4][:], ACT.Copy)\
                        .then_inc(sems["attT_out"], 1)
                if active(i - 3):
                    relu(i - 3, 1)
                if active(i):
                    done(act, "qn_done", i)
                    nc.scalar.activation(stack[:, :, :, 0, :].rearrange("p t h d -> p (t h) d"), qn[:], ACT.Copy)\
                        .then_inc(sems["hi_done"], 1)
                if isinstance(i, int) and i == 1:
                    signs()
                if active(i - 1):
                    done(act, "x1T_tr", i - 1)
                    freed(act, "ratio_done", i - 1)
                    for c in range(NC):
                        nc.scalar.activation(ke[:, 1, c], bank[5][:, c * T * S:(c + 1) * T * S]
                                             .rearrange("p (t s) -> p t s", t=T), ACT.Exp, bias=ln_max[:, 0:1])\
                            .then_inc(sems["ek_done"], 1)
                if active(i - 2):
                    done(act, "x2T_tr", i - 2)
                    freed(act, "up_mm", i - 2)
                    nc.scalar.activation(x2hi[:].rearrange("p c t s -> p (c t s)"), bank[4][:], ACT.Copy)\
                        .then_inc(sems["x2hi_done"], 1)

            pipeline(act, step)

        @block.gpsimd
        def _(pool):
            nc.gpsimd.memset(half_neg[:], -0.5).then_inc(consts_done, 1)
            nc.gpsimd.memset(ln_max[:], -LN_MAX).then_inc(consts_done, 1)
            nc.gpsimd.memset(v_sb[:], 1.0).then_inc(consts_done, 1)
            pool.wait_ge(params_in, PARAMS)
            nc.gpsimd.tensor_copy(id_h[:], id_f[:]).then_inc(consts_done, 1)
            nc.gpsimd.tensor_copy(id_b[:], id_f[:]).then_inc(consts_done, 1)
            nc.gpsimd.memset(mask_f[:], 0.0).then_inc(consts_done, 1)
            pool.wait_ge(consts_done, 6)
            nc.gpsimd.affine_select(out=mask_f[:], in_=mask_f[:], compare_op=ALU.is_ge, fill=pool.to_reg(MASKED),
                                    base=0, pattern=[[0, REP], [1, S]], channel_multiplier=-1).then_inc(consts_done, 1)
            pool.wait_ge(consts_done, 7)
            nc.gpsimd.tensor_copy(mask_sb[:], mask_f[:]).then_inc(consts_done, 1)
            pool.wait_ge(consts_done, 8)
            pool.wait_ge(setup_act, 4)
            pool.wait_ge(setup_dve, 12)

            def inverse_root(n, p):
                done(pool, f"ag{n + 1}", p)
                alone(pool)
                nc.gpsimd.tensor_scalar(veps[n][:], mv[n][:, :, 1], LN_EPS, 1.0, ALU.add, ALU.mult)\
                    .then_inc(sems[f"ve{n + 1}"], 1)
                done(pool, f"ve{n + 1}", p)
                nc.gpsimd.tensor_tensor(rstd[n][:], veps[n][:], half_neg[:, 0:T], ALU.pow)\
                    .then_inc(sems[f"rs{n + 1}"], 1)

            def rope_products(p):
                done(pool, "qk_out", p)
                freed(pool, "rot_done", p)
                half = HD // 2
                c = cos_sb[:].unsqueeze(1).to_broadcast([128, T * NQK, HD])
                nc.gpsimd.tensor_tensor(rope_a[:], qk[:], c, ALU.mult).then_inc(sems["rope_done"], 1)
                for to, of in ((0, half), (half, 0)):
                    s = sin_sb[:, to:to + half].unsqueeze(1).to_broadcast([128, T * NQK, half])
                    nc.gpsimd.tensor_tensor(rope_b[:, :, to:to + half], qk[:, :, of:of + half], s, ALU.mult)\
                        .then_inc(sems["rope_done"], 1)

            def step(i):
                if active(i - 2):
                    done(pool, "rec0_done", i - 2)
                    nc.gpsimd.tensor_tensor(newt[:], ratio[:, 1], rec0[:], ALU.mult).then_inc(sems["newt_done"], 1)
                if active(i - 1):
                    done(pool, "x_in", i - 1)
                    freed(pool, "r1_done", i - 1)
                    nc.gpsimd.tensor_tensor(xb_sb[:], x_sb[:], bo_b[:].unsqueeze(1).to_broadcast([128, T, D]), ALU.add)\
                        .then_inc(sems["xb_done"], 1)
                if active(i - 2):
                    done(pool, "nrec_done", i - 2)
                    nc.gpsimd.tensor_tensor(ny[:], ratio[:, 0], nrec[:], ALU.mult).then_inc(sems["ny_done"], 1)
                if active(i):
                    rope_products(i)
                if active(i - 2):
                    inverse_root(1, i - 2)
                if active(i - 1):
                    inverse_root(0, i - 1)
                    p = i - 1
                    done(pool, "ctx_in", p)
                    done(pool, "ek_done", p)
                    nc.gpsimd.tensor_tensor(ke[:, 0], ke[:, 1], ctxT_sb[:], ALU.mult).then_inc(sems["kv_done"], 1)
                    done(pool, "kv_done", p)
                    freed(pool, "ratio_done", p)
                    for c in range(NC):
                        alone(pool)
                        nc.gpsimd.tensor_scalar(now[:, :, c].rearrange("p a t s -> p a (t s)"),
                                                ke[:, :, c].rearrange("p a t s -> p a (t s)"),
                                                e_now[:, c:c + 1], 1.0, ALU.mult, ALU.mult).then_inc(sems["now_done"], 1)
                if active(i - 3):
                    done(pool, "o3_done", i - 3)
                    done(pool, "kept", i - 3)
                    nc.gpsimd.tensor_tensor(r3[:], o3[:], x2_keep[:], ALU.add).then_inc(sems["r3_done"], 1)
                    inverse_root(2, i - 3)

            pipeline(pool, step)

        @block.vector
        def _(dve):
            dve.wait_ge(params_in, PARAMS)
            nc.vector.tensor_scalar(u_pos[:], tfirst[:], 0.0, None, ALU.max).then_inc(setup_dve, 1)
            nc.vector.tensor_scalar(u_neg[:], tfirst[:], 0.0, None, ALU.min).then_inc(setup_dve, 1)
            nc.vector.memset(dec_sb[:], 1.0).then_inc(setup_dve, 1)
            nc.vector.memset(state[:], 0.0).then_inc(setup_dve, 1)
            nc.vector.tensor_scalar(ups_pow[:].bitcast(I32), ups_sb[:].bitcast(I32), 0x7F800000, None, ALU.bitwise_and)\
                .then_inc(setup_dve, 1)
            nc.vector.tensor_scalar(ups_man[:].bitcast(I32), ups_sb[:].bitcast(I32), -0x7F800001, 0x3F800000,
                                    ALU.bitwise_and, ALU.bitwise_or).then_inc(setup_dve, 1)
            nc.vector.tensor_scalar(dsc_b[:], dsc_b[:], osc_b[:, 0:1], None, ALU.mult).then_inc(setup_dve, 1)
            nc.vector.memset(gain_b[:], -0.5).then_inc(setup_dve, 1)
            dve.wait_ge(setup_dve, 8)
            nc.vector.tensor_scalar(gain_b[:, :, 0:H], gain_in[:], -0.5 * HD ** -0.5, None, ALU.mult).then_inc(setup_dve, 1)
            dve.wait_ge(setup_act, 2)
            dve.wait_ge(setup_dve, 9)
            for c in range(NC):
                nc.vector.tensor_scalar(dec_sb[:, :, c].rearrange("p a t s -> p a (t s)"),
                                        dec_sb[:, :, c].rearrange("p a t s -> p a (t s)"),
                                        tdec[:, c:c + 1], None, ALU.mult).then_inc(setup_dve, 1)
            dve.wait_ge(setup_dve, 11)
            nc.vector.memset(dec_sb[:].rearrange("p a c t s -> p (a c t) s")[:, :, 0:1], 0.0).then_inc(setup_dve, 1)
            dve.wait_ge(setup_dve, 12)
            dve.wait_ge(consts_done, 8)

            def attend_norm(p, t):
                done(dve, "un_tr", p, t + 1)
                o = bank[4 - 2 * t][:].rearrange("p (j g d) -> p j g d", j=REP, g=KVH)
                nc.vector.reciprocal(prec[:, t].rearrange("p (j g) -> p j g", j=REP), o[:, :, :, HD])\
                    .then_inc(sems["prec_done"], 1)
                done(dve, "prec_done", p, t + 1)
                freed(dve, "attT_tr", p)
                nc.vector.tensor_tensor(att[:, t].rearrange("p (g j) d -> p j g d", g=KVH), o[:, :, :, 0:HD],
                                        prec[:, t].rearrange("p (j g) -> p j g", j=REP).unsqueeze(3)
                                        .to_broadcast([128, REP, KVH, HD]), ALU.mult).then_inc(sems["att_done"], 1)

            def moments(n, p, rows):
                for t in range(T):
                    nc.vector.bn_stats(stats[n][:, t], rows[:, t, :]).then_inc(sems[f"bn{n + 1}"], 1)
                for t in range(T):
                    done(dve, f"bn{n + 1}", p, t + 1)
                    alone(dve)
                    nc.vector.bn_aggr(mv[n][:, t], stats[n][:, t]).then_inc(sems[f"ag{n + 1}"], 1)

            def normed(n, p, rows, to, name):
                done(dve, f"rs{n + 1}", p)
                for t in range(T):
                    nc.vector.tensor_scalar(to[:, t], rows[:, t, :], mv[n][:, t, 0:1], rstd[n][:, t:t + 1],
                                            ALU.subtract, ALU.mult).then_inc(sems[name], 1)

            W = NC * T * S

            def scan(p):
                done(dve, "now_done", p)
                nc.vector.tensor_tensor_scan(state[:, 1:2 * W + 1], dec_sb[:].rearrange("p a c t s -> p (a c t s)"),
                                             ke[:].rearrange("p a c t s -> p (a c t s)"), 0.0, ALU.mult, ALU.add)\
                    .then_inc(sems["scan_done"], 1)
                done(dve, "scan_done", p)
                nc.vector.tensor_copy(state[:, 0:2 * W].rearrange("p (n s) -> p n s", s=S)[:, :, 0:1],
                                      ke[:].rearrange("p a c t s -> p (a c t) s")[:, :, 0:1]).then_inc(sems["fix_done"], 1)
                done(dve, "fix_done", p)
                for c in range(NC):
                    nc.vector.scalar_tensor_tensor(
                        ratio[:, :, c].rearrange("p a t s -> p a (t s)"),
                        state[:, 0:2 * W].rearrange("p (a c n) -> p a c n", a=2, c=NC)[:, :, c, :],
                        e_state[:, c:c + 1], now[:, :, c].rearrange("p a t s -> p a (t s)"),
                        ALU.mult, ALU.add).then_inc(sems["ratio_done"], 1)

            def down_weights():
                dve.wait_ge(setup_act, 5)
                for j in range(NJ):
                    nc.vector.tensor_scalar(dn_sb[:, j], dn_f[:, j], ups_pow[:, j:j + 1], None, ALU.mult)\
                        .then_inc(signs_done, 1)

            def newton_rms(p):
                done(dve, "y0_done", p)
                nc.vector.tensor_tensor(ysq[:], y0[:], y0[:], ALU.mult).then_inc(sems["ysq_done"], 1)
                done(dve, "ysq_done", p)
                nc.vector.tensor_tensor(vy[:], ysq[:], msq[:], ALU.mult).then_inc(sems["vy_done"], 1)
                done(dve, "vy_done", p)
                nc.vector.scalar_tensor_tensor(ny0[:], vy[:], 3.0, y0[:], ALU.subtract, ALU.mult)\
                    .then_inc(sems["ny0_done"], 1)
                done(dve, "ny0_done", p)
                nc.vector.tensor_tensor(rscale[:], ny0[:], gain_b[:].rearrange("p t h -> p (t h)"), ALU.mult)\
                    .then_inc(sems["rscale_done"], 1)

            def low_bits(p, ns):
                for n in ns:
                    done(dve, "hidhi_done", p, n + 1)
                    nc.vector.tensor_tensor(hid_lo[:, 2 * n:2 * n + 2], hid[:, 2 * n:2 * n + 2],
                                            hid_hi[:, 2 * n:2 * n + 2], ALU.subtract).then_inc(sems["hidlo_done"], 1)

            def fill_stack(p):
                done(dve, "hi_done", p)
                nc.vector.tensor_tensor(stack[:, :, :, 1, :].rearrange("p t h d -> p (t h) d"), qn[:],
                                        stack[:, :, :, 0, :].rearrange("p t h d -> p (t h) d"), ALU.subtract)\
                    .then_inc(sems["lo_done"], 1)
                done(dve, "lo_done", p)
                nc.vector.tensor_copy(stack[:, :, 0:H, 2:4, :].rearrange("p t h r d -> p t h (r d)"),
                                      stack[:, :, 0:H, 0:2, :].rearrange("p t h r d -> p t h (r d)"))\
                    .then_inc(sems["stack_done"], 1)
                for to, of in ((2, 1), (3, 0)):
                    nc.vector.tensor_copy(stack[:, :, H:NQK, to, :], stack[:, :, H:NQK, of, :])\
                        .then_inc(sems["stack_done"], 1)

            z = bank[0][:].rearrange("p (t d) -> p t d", t=T)

            def step(i):
                if active(i - 1):
                    p = i - 1
                    done(dve, "qT_tr", p)
                    freed(dve, "scores_mm", p)
                    nc.vector.tensor_copy(qT_sb[:, 1].rearrange("p b s -> p (b s)"), bank[3].bitcast(F16)[:])\
                        .then_inc(sems["q1_out"], 1)
                if active(i - 2):
                    scan(i - 2)
                if active(i - 1):
                    attend_norm(i - 1, 0)
                if active(i - 3):
                    low_bits(i - 3, (0, 1))
                if active(i):
                    done(dve, "qkv_mm", i)
                    for t in range(T):
                        ins = nc.vector.tensor_tensor(qk[:, t * NQK:(t + 1) * NQK, :].rearrange("p h d -> p (h d)"),
                                                      bank[3 * t][:, 0:NQK * HD], bqk_b[:, 0:NQK * HD], ALU.add)
                    ins.then_inc(sems["qk_out"], 1)
                if active(i - 2):
                    p = i - 2
                    done(dve, "newt_done", p)
                    nc.vector.scalar_tensor_tensor(nrec[:], newt[:], 2.0, rec0[:], ALU.subtract, ALU.mult)\
                        .then_inc(sems["nrec_done"], 1)
                if active(i):
                    done(dve, "sq_done", i)
                    nc.vector.tensor_reduce(ssum[:], sq[:], AX_X, ALU.add).then_inc(sems["ssum_done"], 1)
                    done(dve, "ssum_done", i)
                    nc.vector.tensor_scalar(msq[:], ssum[:], 1.0 / HD, RMS_EPS, ALU.mult, ALU.add)\
                        .then_inc(sems["msq_done"], 1)
                if active(i - 1):
                    attend_norm(i - 1, 1)
                if active(i):
                    for t in range(T):
                        ins = nc.vector.tensor_tensor(v_sb[:, t, :, 0:HD],
                                                      bank[3 * t][:, NQK * HD:E].rearrange("p (g d) -> p g d", g=KVH),
                                                      bqk_b[:, NQK * HD:E].rearrange("p (g d) -> p g d", g=KVH), ALU.add)
                    ins.then_inc(sems["v_out"], 1)
                if active(i - 2):
                    p = i - 2
                    done(dve, "ny_done", p)
                    freed(dve, "zT_tr", p)
                    nc.vector.tensor_tensor(zT[:].rearrange("p c t s -> p (c t s)"), bank[5][:],
                                            ny[:].rearrange("p c t s -> p (c t s)"), ALU.subtract)\
                        .then_inc(sems["z_done"], 1)
                if active(i):
                    newton_rms(i)
                if active(i - 3):
                    low_bits(i - 3, (2,))
                if active(i - 2):
                    done(dve, "zT_tr", i - 2)
                    moments(1, i - 2, z)
                if active(i - 1):
                    p = i - 1
                    done(dve, "wo_mm", p)
                    done(dve, "xb_done", p)
                    nc.vector.tensor_tensor(r1[:].rearrange("p t d -> p (t d)"), bank[2][:],
                                            xb_sb[:].rearrange("p t d -> p (t d)"), ALU.add).then_inc(sems["r1_done"], 1)
                    done(dve, "r1_done", p)
                    moments(0, p, r1)
                if active(i - 3):
                    low_bits(i - 3, (3,))
                if active(i - 2):
                    freed(dve, "x2T_tr", i - 2)
                    freed(dve, "kept", i - 2)
                    normed(1, i - 2, z, x2, "x2_done")
                if active(i):
                    done(dve, "rope_done", i)
                    nc.vector.tensor_tensor(rot[:], rope_a[:], rope_b[:], ALU.add).then_inc(sems["rot_done"], 1)
                if active(i - 1):
                    freed(dve, "x1T_tr", i - 1)
                    normed(0, i - 1, r1, x1, "x1_done")
                if active(i):
                    done(dve, "rot_done", i)
                    nc.vector.tensor_tensor(qn[:], rot[:], rscale[:].unsqueeze(2).to_broadcast([128, T * NQK, HD]),
                                            ALU.mult).then_inc(sems["qn_done"], 1)
                    fill_stack(i)
                if isinstance(i, int) and i == 1:
                    down_weights()
                if active(i - 2):
                    done(dve, "x2hi_done", i - 2)
                    nc.vector.tensor_tensor(x2lo[:].rearrange("p c t s -> p (c t s)"), bank[4][:],
                                            x2hi[:].rearrange("p c t s -> p (c t s)"), ALU.subtract)\
                        .then_inc(sems["x2lo_done"], 1)
                if active(i - 3):
                    p = i - 3
                    done(dve, "dn_mm", p)
                    freed(dve, "r3_done", p)
                    nc.vector.tensor_tensor(o3[:], bank[1][:].rearrange("p (t d) -> p t d", t=T),
                                            dsc_b[:].unsqueeze(1).to_broadcast([128, T, D]), ALU.mult)\
                        .then_inc(sems["o3_done"], 1)
                    done(dve, "r3_done", p)
                    moments(2, p, r3)
                    freed(dve, "stored", p)
                    normed(2, p, r3, outb, "out_done")

            pipeline(dve, step)


def kernel(x, ctx_2048, L0_attn_Wq, L0_attn_bq, L0_attn_Wk, L0_attn_bk, L0_attn_Wv, L0_attn_bv, L0_attn_Wo,
           L0_attn_bo, L0_attn_q_gain, L0_xattn_time_decay, L0_xattn_time_first, L0_ffn_up_weight,
           L0_ffn_down_weight, L0_ffn_up_scale, L0_ffn_down_scale, L0_ffn_output_scale):
    import concourse.bacc as bacc
    from concourse.bass_utils import run_bass_kernel_spmd

    def a(v):
        return np.asarray(v)

    order = np.arange(H).reshape(2, 2, REP).transpose(0, 2, 1).reshape(H)
    wq = a(L0_attn_Wq).reshape(H, HD, D)[order].reshape(D, D)
    bq = a(L0_attn_bq).reshape(H, HD)[order].reshape(D)

    def chunked(w):
        return np.ascontiguousarray(w.reshape(-1, 128, w.shape[1]).transpose(1, 0, 2))

    def to_channels(v):
        return np.ascontiguousarray(a(v).reshape(PAIRS, T, S, NC, 128).transpose(0, 4, 3, 1, 2))

    inv_freq = (np.float32(1.0) / np.float32(10000.0) ** (np.arange(0, HD, 2, dtype=np.float32) / np.float32(HD)))
    freqs = np.outer(np.arange(S, dtype=np.float32), inv_freq.astype(np.float32)).astype(np.float32)
    cos, sin = np.cos(freqs), np.sin(freqs)

    arrays = {
        "x": np.ascontiguousarray(a(x).reshape(PAIRS, T, S, D).transpose(0, 2, 1, 3)),
        "xT": to_channels(x),
        "ctxT": to_channels(ctx_2048),
        "wqkv": chunked(np.concatenate([wq, a(L0_attn_Wk), a(L0_attn_Wv)]).T),
        "bqkv": np.concatenate([bq, a(L0_attn_bk), a(L0_attn_bv)]),
        "gains": a(L0_attn_q_gain)[order],
        "wo": chunked(a(L0_attn_Wo).T),
        "bo": a(L0_attn_bo),
        "decay_in": np.ascontiguousarray(a(L0_xattn_time_decay).reshape(NC, 128).T),
        "first_in": np.ascontiguousarray(a(L0_xattn_time_first).reshape(NC, 128).T),
        "up": chunked(a(L0_ffn_up_weight).T),
        "down": chunked(a(L0_ffn_down_weight).T),
        "up_s": np.ascontiguousarray(a(L0_ffn_up_scale).reshape(NJ, 128).T),
        "down_s": a(L0_ffn_down_scale),
        "out_s": a(L0_ffn_output_scale),
        "rope_cos": np.concatenate([cos, cos], 1).astype(np.float32),
        "rope_sin": np.concatenate([sin, -sin], 1).astype(np.float32),
        "ident_in": np.eye(128, dtype=np.float32),
    }
    nc = bacc.Bacc("TRN2", target_bir_lowering=False, num_devices=1)
    args = [nc.dram_tensor(f"{n}_dram", v.shape, F32, kind="ExternalInput").ap() for n, v in arrays.items()]
    result = nc.dram_tensor("out_dram", (PAIRS, S, T, D), F32, kind="ExternalOutput").ap()
    build(nc, *args, result)
    r = run_bass_kernel_spmd(nc, [{f"{n}_dram": v for n, v in arrays.items()}], core_ids=[0])
    got = r.results[0]["out_dram"]
    return np.ascontiguousarray(got.reshape(PAIRS, S, T, D).transpose(0, 2, 1, 3)).reshape(B, S, D)
```

```python
from contextlib import ExitStack

import numpy as np

import concourse.bass as bass
from concourse import mybir

ALU = mybir.AluOpType
ACT = mybir.ActivationFunctionType
F32 = mybir.dt.float32
F16 = mybir.dt.float16
BF16 = mybir.dt.bfloat16
I32 = mybir.dt.int32
AX_X = mybir.AxisListType.X

B, S, D = 16, 128, 256
H, KVH = 16, 4
HD = D // H
KVD = KVH * HD
NQK = H + KVH
DFF = 1024
T = 2
PAIRS = B // T
NC = D // 128
NJ = DFF // 128
E = D + 2 * KVD
REP = H // KVH
VW = 32
MASKED = -1e30
BLOCKS = NQK // 2
QBLOCKS = H // 2
RMS_EPS = 1.1920929e-07
LN_EPS = 1e-5
LN_MAX = float(D) ** 0.5
GAIN_LIMIT = 16.0
DEPTH = 4
PEELED = DEPTH + 1


def first(p):
    return isinstance(p, int) and p == 0


def active(p):
    return not isinstance(p, int) or 0 <= p < PAIRS


def build(nc, x, xT, ctxT, wqkv, bqkv, gains, wo, bo, decay_in, first_in, up, down, up_s, down_s, out_s,
          rope_cos, rope_sin, ident_in, out):
    with ExitStack() as ctx:
        def sb(name, shape, dt=F32):
            return ctx.enter_context(nc.sbuf_tensor(name, shape, dt))

        def sem(name):
            return ctx.enter_context(nc.semaphore(name))

        bank = [ctx.enter_context(nc.psum_tensor(f"bank{n}", [128, 512], F32)) for n in range(8)]
        ring = [bank[6], bank[7]]

        wqkv_sb = sb("wqkv_sb", [128, NC, E])
        wo_sb = sb("wo_sb", [128, NC, D])
        bqk_b = sb("bqk_b", [128, E])
        gain_in = sb("gain_in", [128, T, H])
        gain_b = sb("gain_b", [128, T, NQK])
        bo_b = sb("bo_b", [128, D])
        dsc_b = sb("dsc_b", [128, D])
        osc_b = sb("osc_b", [128, 1])
        cos_sb = sb("cos_sb", [128, HD])
        sin_sb = sb("sin_sb", [128, HD])
        id_f = sb("id_f", [128, 128])
        id_h = sb("id_h", [128, 128], F16)
        id_b = sb("id_b", [128, 128], BF16)
        gain_sq = sb("gain_sq", [128, H])
        gain_top = sb("gain_top", [128, 1])
        guard = sb("guard", [128, 1], I32)
        mask_f = sb("mask_f", [128, REP, S])
        mask_sb = sb("mask_sb", [128, REP, S], BF16)
        up_f = sb("up_f", [128, NC, DFF])
        up_sb = sb("up_sb", [128, NC, DFF], F16)
        dn_f = sb("dn_f", [128, NJ, D])
        dn_sb = sb("dn_sb", [128, NJ, D], BF16)
        ups_sb = sb("ups_sb", [128, NJ])
        ups_pow = sb("ups_pow", [128, NJ])
        ups_man = sb("ups_man", [128, NJ])
        tdec = sb("tdec", [128, NC])
        tdec2 = sb("tdec2", [128, NC])
        tfirst = sb("tfirst", [128, NC])
        e_state = sb("e_state", [128, NC])
        e_now = sb("e_now", [128, NC])
        u_neg = sb("u_neg", [128, NC])
        u_pos = sb("u_pos", [128, NC])
        dec_sb = sb("dec_sb", [128, 2, NC, T, S])
        half_neg = sb("half_neg", [128, T * NQK])
        ln_max = sb("ln_max", [128, 1])

        xT_sb = sb("xT_sb", [128, NC, T, S])
        x_sb = sb("x_sb", [128, T, D])
        ctxT_sb = sb("ctxT_sb", [128, NC, T, S])
        xb_sb = sb("xb_sb", [128, T, D])
        qk = sb("qk", [128, T * NQK, HD])
        v_new = sb("v_new", [128, T, KVH, HD])
        v_sb = sb("v_sb", [128, T, KVH, VW])
        sq = sb("sq", [128, T * NQK, HD])
        ssum = sb("ssum", [128, T * NQK])
        msq = sb("msq", [128, T * NQK])
        lnms = sb("lnms", [128, T * NQK])
        y0 = sb("y0", [128, T * NQK])
        ysq = sb("ysq", [128, T * NQK])
        vy = sb("vy", [128, T * NQK])
        ny0 = sb("ny0", [128, T * NQK])
        rscale = sb("rscale", [128, T * NQK])
        rope_a = sb("rope_a", [128, T * NQK, HD])
        rope_b = sb("rope_b", [128, T * NQK, HD])
        rot = sb("rot", [128, T * NQK, HD])
        qn = sb("qn", [128, T * NQK, HD])
        stack = sb("stack", [128, T, NQK, 4, HD], F16)
        qT_sb = sb("qT_sb", [128, T, QBLOCKS, 128], F16)
        kT_sb = sb("kT_sb", [128, T, 2, 128], F16)
        maskq_f = sb("maskq_f", [128, REP, S])
        maskq_sb = sb("maskq_sb", [128, REP, S], BF16)
        row_max = sb("row_max", [128, T * KVH, REP])
        shift = sb("shift", [T * H, S])
        probs = sb("probs", [128, KVH, REP, 128])
        prec = sb("prec", [128, T, H])
        att_un = sb("att_un", [128, T, REP, S])
        att = sb("att", [128, T, H, HD])
        attT_sb = sb("attT_sb", [128, NC, T, 128])
        r1 = sb("r1", [128, T, D])
        x1 = sb("x1", [128, T, D])
        stats = [sb(f"stats{n}", [128, T, 6]) for n in range(3)]
        mv = [sb(f"mv{n}", [128, T, 2]) for n in range(3)]
        veps = [sb(f"veps{n}", [128, T]) for n in range(3)]
        rstd = [sb(f"rstd{n}", [128, T]) for n in range(3)]
        ke = sb("ke", [128, 2, NC, T, S])
        state = sb("state", [128, 2 * NC * T * S + 2])
        now = sb("now", [128, 2, NC, T, S])
        ratio = sb("ratio", [128, 2, NC, T, S])
        lnden = sb("lnden", [128, NC, T, S])
        rec0 = sb("rec0", [128, NC, T, S])
        newt = sb("newt", [128, NC, T, S])
        guess = sb("guess", [128, NC, T, S])
        ny = sb("ny", [128, NC, T, S])
        zT = sb("zT", [128, NC, T, S])
        x2 = sb("x2", [128, T, D])
        x2_keep = sb("x2_keep", [128, T, D])
        x2hi = sb("x2hi", [128, NC, T, S], F16)
        x2lo = sb("x2lo", [128, NC, T, S], F16)
        hid = sb("hid", [128, NJ, T * S])
        hid_hi = sb("hid_hi", [128, NJ, T * S], F16)
        hid_lo = sb("hid_lo", [128, NJ, T * S], F16)
        o3 = sb("o3", [128, T, D])
        r3 = sb("r3", [128, T, D])
        outb = sb("outb", [128, T, D])

        names = dict(
            xT_in=16, x_in=16, ctx_in=16, stored=16,
            qkv_mm=2, kT_tr=1, qT_tr=2, scores_mm=8, pv_mm=8, attT_tr=1, wo_mm=1, x1T_tr=1, zT_tr=1,
            x2T_tr=1, rows_mm=8, rows_max=8, max_tr=1, shift_done=1, un_out=2, un_tr=2, up_mm=4, dn_mm=2,
            qk_out=1, v_out=1, sq_done=1, ssum_done=1, msq_done=1, rscale_done=1, rope_done=3, v_ready=1, ln_rms=1, y0_done=1, ysq_done=1, vy_done=1, ny0_done=1,
            rot_done=1, qn_done=1, hi_done=1, lo_done=1, stack_done=3, kT_out=1, q0_out=1, q1_out=1,
            probs_done=8, prec_done=2, att_done=2, attT_out=1, xb_done=1, r1_done=1, bn1=2, ag1=2, ve1=1,
            rs1=1, x1_done=2, ek_done=2, kv_done=1, now_done=2, scan_done=1, fix_done=1, ratio_done=2,
            ln_done=1, rec0_done=1, guess_done=2, ny_done=1, z_done=1, bn2=2, ag2=2, ve2=1,
            rs2=1, x2_done=2, kept=16, x2hi_done=1, x2lo_done=1, hid_done=8, hidhi_done=4, lo2_done=1, hidlo_done=3,
            o3_done=1, r3_done=1, bn3=2, ag3=2, ve3=1, rs3=1, out_done=2)
        sems = {n: sem(n) for n in names}
        project_in = sem("project_in")
        norm_in = sem("norm_in")
        params_in = sem("params_in")
        ffn_in = sem("ffn_in")
        signs_done = sem("signs_done")
        consts_done = sem("consts_done")
        setup_dve = sem("setup_dve")
        setup_act = sem("setup_act")

        def done(eng, name, p, k=None):
            eng.wait_ge(sems[name], p * names[name] + (names[name] if k is None else k))

        def freed(eng, name, p, back=1, k=None):
            if not (isinstance(p, int) and p < back):
                done(eng, name, p - back, k)

        def alone(eng):
            eng.nop(nofuse=True)

        project_consts = [(wqkv_sb[:], wqkv), (bqk_b[:], bqkv.partition_broadcast(128))]
        norm_consts = [(cos_sb[:], rope_cos), (sin_sb[:], rope_sin),
                       (gain_in[:, 0, :], gains.partition_broadcast(128)),
                       (gain_in[:, 1, :], gains.partition_broadcast(128))]
        consts = [(id_f[:], ident_in), (wo_sb[:], wo), (tdec[:], decay_in), (tfirst[:], first_in), (ups_sb[:], up_s),
                  (bo_b[:], bo.partition_broadcast(128)),
                  (dsc_b[:], down_s.partition_broadcast(128)), (osc_b[:], out_s.partition_broadcast(128))]
        PROJECT_IN = 16 * len(project_consts)
        NORM_IN = 16 * len(norm_consts)
        PARAMS = 16 * len(consts)

        MIXER_IN = 5

        block = ctx.enter_context(nc.Block())

        def pipeline(eng, step, last_extra=0):
            for i in range(PEELED):
                step(i)
            with eng.Fori(PEELED, PAIRS) as i:
                step(i)
            for i in range(PAIRS, PAIRS + DEPTH):
                step(i)

        @block.sync
        def _(sp):
            sp.dma_start(xT_sb[:], xT[0]).then_inc(sems["xT_in"], 16)
            for dst, src in project_consts:
                sp.dma_start(dst, src).then_inc(project_in, 16)
            for dst, src in norm_consts:
                sp.dma_start(dst, src).then_inc(norm_in, 16)
            for dst, src in consts:
                sp.dma_start(dst, src).then_inc(params_in, 16)
            sp.dma_start(x_sb[:], x[0]).then_inc(sems["x_in"], 16)
            sp.dma_start(ctxT_sb[:], ctxT[0]).then_inc(sems["ctx_in"], 16)
            sp.dma_start(up_f[:], up).then_inc(ffn_in, 16)
            sp.dma_start(dn_f[:], down).then_inc(ffn_in, 16)

            def step(i):
                if active(i - 2) and (not isinstance(i, int) or i - 1 < PAIRS):
                    done(sp, "kv_done", i - 2)
                    sp.dma_start(ctxT_sb[:], ctxT[i - 1]).then_inc(sems["ctx_in"], 16)
                if not isinstance(i, int) or i + 1 < PAIRS:
                    done(sp, "qkv_mm", i)
                    sp.dma_start(xT_sb[:], xT[i + 1]).then_inc(sems["xT_in"], 16)
                if active(i - 3):
                    done(sp, "x2_done", i - 3)
                    freed(sp, "r3_done", i - 3)
                    sp.dma_start(x2_keep[:], x2[:]).then_inc(sems["kept"], 16)
                if active(i - 4):
                    done(sp, "out_done", i - 4)
                    sp.dma_start(out[i - 4], outb[:]).then_inc(sems["stored"], 16)
                if not isinstance(i, int) or 1 <= i < PAIRS:
                    done(sp, "xb_done", i - 1)
                    sp.dma_start(x_sb[:], x[i]).then_inc(sems["x_in"], 16)

            for i in range(PEELED):
                step(i)
            with sp.Fori(PEELED, PAIRS - 1) as i:
                step(i)
            for i in range(PAIRS - 1, PAIRS + DEPTH):
                step(i)
            sp.wait_ge(sems["stored"], 16 * PAIRS)

        @block.tensor
        def _(pe):
            pe.wait_ge(project_in, PROJECT_IN)

            def heads_to_rows(p):
                done(pe, "stack_done", p)
                freed(pe, "attT_out", p)
                for t in range(T):
                    for b in range(2):
                        mm = nc.tensor.transpose(bank[4].bitcast(F16)[:, (2 * t + b) * 128:(2 * t + b + 1) * 128],
                                                 stack[:, t, H + 2 * b:H + 2 * b + 2, :, :].rearrange("p h r d -> p (h r d)"),
                                                 id_h[:])
                mm.then_inc(sems["kT_tr"], 1)
                for t in (1, 0):
                    freed(pe, "hid_done", p, 3, k=6 + 2 * t)
                    for b in range(QBLOCKS):
                        mm = nc.tensor.transpose(bank[3 * t].bitcast(F16)[:, b * 128:(b + 1) * 128],
                                                 stack[:, t, 2 * b:2 * b + 2, :, :].rearrange("p h r d -> p (h r d)"),
                                                 id_h[:])
                    mm.then_inc(sems["qT_tr"], 1)

            def row_scores(p):
                done(pe, "kT_out", p)
                done(pe, "q0_out", p)
                done(pe, "q1_out", p)
                freed(pe, "r1_done", p)
                for n in range(T * KVH):
                    t, g = n // KVH, n % KVH
                    if n >= 1:
                        done(pe, "rows_max", p, n)
                    r = 64 * (g % 2)
                    nc.tensor.matmul(bank[2][:], id_b[:], maskq_sb[:].rearrange("p j s -> p (j s)"),
                                     start=True, stop=False)
                    for j in range(REP):
                        mm = nc.tensor.matmul(bank[2][:, j * S:(j + 1) * S], qT_sb[r:r + 64, t, 4 * (g // 2) + j, :],
                                              kT_sb[r:r + 64, t, g // 2, :], start=False, stop=(j == REP - 1))
                    mm.then_inc(sems["rows_mm"], 1)
                done(pe, "rows_max", p)
                nc.tensor.transpose(bank[2][0:T * H, 0:S], row_max[:].rearrange("p n j -> p (n j)"), id_f[:])\
                    .then_inc(sems["max_tr"], 1)
                done(pe, "shift_done", p)

            def scores(p, n, guarded):
                t, g = n // KVH, n % KVH
                if n == 0:
                    done(pe, "kT_out", p)
                if g == 0:
                    done(pe, f"q{t}_out", p)
                if n >= 2:
                    done(pe, "probs_done", p, n - 1)
                else:
                    freed(pe, "probs_done", p, k=T * KVH - 1 + n)
                r = 64 * (g % 2)
                nc.tensor.matmul(ring[n % 2][:], kT_sb[r:r + 64, t, g // 2, :],
                                 qT_sb[r:r + 64, t, 4 * (g // 2):4 * (g // 2) + 4, :].rearrange("p a b -> p (a b)"),
                                 start=True, stop=False)
                mm = nc.tensor.matmul(ring[n % 2][:], id_b[:], mask_sb[:].rearrange("p j s -> p (j s)"),
                                      start=False, stop=not guarded)
                if guarded:
                    for j in range(REP):
                        h = n * REP + j
                        mm = nc.tensor.matmul(ring[n % 2][:, j * S:(j + 1) * S],
                                              id_f[0:T * H, h:h + 1].to_broadcast([T * H, S]), shift[:],
                                              start=False, stop=(j == REP - 1))
                mm.then_inc(sems["scores_mm"], 1)

            def products(p, n):
                t, g = n // KVH, n % KVH
                if n == 0:
                    done(pe, "v_ready", p)
                    freed(pe, "x2lo_done", p, 2)
                elif n == KVH:
                    freed(pe, "r1_done", p)
                done(pe, "probs_done", p, n + 1)
                r = VW * g
                nc.tensor.matmul(bank[4 - 2 * t][r:r + VW, :], v_sb[:, t, g, :],
                                 probs[:, g].rearrange("p j s -> p (j s)"),
                                 start=True, stop=True).then_inc(sems["pv_mm"], 1)

            def attention_to_tokens(p, t):
                done(pe, "un_out", p, t + 1)
                for j in range(REP):
                    mm = nc.tensor.transpose(bank[4 - 2 * t][:, j * 128:(j + 1) * 128], att_un[:, t, j, :], id_f[:])
                mm.then_inc(sems["un_tr"], 1)

            def project(p):
                done(pe, "xT_in", p)
                for t in range(T):
                    if not first(p):
                        done(pe, f"q{t}_out", p - 1)
                    for c in range(NC):
                        mm = nc.tensor.matmul(bank[3 * t][:, 0:E], xT_sb[:, c, t, :], wqkv_sb[:, c, :],
                                              start=(c == 0), stop=(c == NC - 1))
                    mm.then_inc(sems["qkv_mm"], 1)

            def attention_to_channels(p):
                done(pe, "att_done", p)
                a = att[:].rearrange("p t h d -> p t (h d)")
                for c in range(NC):
                    for t in range(T):
                        mm = nc.tensor.transpose(bank[4][:, (2 * c + t) * 128:(2 * c + t + 1) * 128],
                                                 a[:, t, c * 128:(c + 1) * 128], id_f[:])
                mm.then_inc(sems["attT_tr"], 1)

            def project_out(p):
                done(pe, "attT_out", p)
                for t in range(T):
                    for c in range(NC):
                        mm = nc.tensor.matmul(bank[2][:, t * D:(t + 1) * D], attT_sb[:, c, t, :], wo_sb[:, c, :],
                                              start=(c == 0), stop=(c == NC - 1))
                mm.then_inc(sems["wo_mm"], 1)

            def mixed_to_tokens(p):
                done(pe, "z_done", p)
                for t in range(T):
                    for c in range(NC):
                        mm = nc.tensor.transpose(bank[5][:, t * D + c * 128:t * D + (c + 1) * 128], zT[:, c, t, :], id_f[:])
                mm.then_inc(sems["zT_tr"], 1)

            def ffn_up(p, i, n):
                if n == 0:
                    done(pe, "x2hi_done", p)
                    done(pe, "x2lo_done", p)
                if n >= 2:
                    done(pe, "hid_done", p, 2 * (n - 1))
                elif active(i):
                    done(pe, "v_out", i)
                elif active(i - 1):
                    done(pe, f"q{n}_out", i - 1)
                else:
                    freed(pe, "hid_done", p, k=2 * (n + 3))
                for s in range(2):
                    j = 2 * n + s
                    m = 0
                    for c in range(NC):
                        for part in (x2hi, x2lo):
                            mm = nc.tensor.matmul(bank[3 * (n % 2)][:, s * T * S:(s + 1) * T * S],
                                                  up_sb[:, c, j * 128:(j + 1) * 128],
                                                  part[:, c, :, :].rearrange("p t s -> p (t s)"),
                                                  start=(m == 0), stop=(m == 2 * NC - 1))
                            m += 1
                mm.then_inc(sems["up_mm"], 1)

            def x1_to_channels(p):
                done(pe, "x1_done", p)
                freed(pe, "x2_done", p)
                for c in range(NC):
                    for t in range(T):
                        mm = nc.tensor.transpose(bank[5][:, (2 * c + t) * 128:(2 * c + t + 1) * 128],
                                                 x1[:, t, c * 128:(c + 1) * 128], id_f[:])
                mm.then_inc(sems["x1T_tr"], 1)

            def x2_to_channels(p, i):
                done(pe, "x2_done", p)
                if active(i - 1):
                    done(pe, "kT_out", i - 1)
                elif active(i - 2):
                    done(pe, "attT_out", i - 2)
                else:
                    freed(pe, "x2lo_done", p)
                for c in range(NC):
                    for t in range(T):
                        mm = nc.tensor.transpose(bank[4][:, (2 * c + t) * 128:(2 * c + t + 1) * 128],
                                                 x2[:, t, c * 128:(c + 1) * 128], id_f[:])
                mm.then_inc(sems["x2T_tr"], 1)

            def ffn_down(p, t):
                if t == 0:
                    freed(pe, "o3_done", p)
                for j in range(NJ):
                    if t == 0 and j % 2 == 0:
                        done(pe, "hidhi_done", p, j // 2 + 1)
                        if j == 4:
                            done(pe, "lo2_done", p)
                        else:
                            done(pe, "hidlo_done", p, (1, 2, 2, 3)[j // 2])
                    for m, part in enumerate((hid_hi, hid_lo)):
                        mm = nc.tensor.matmul(bank[1][:, t * D:(t + 1) * D], part[:, j, t * S:(t + 1) * S],
                                              dn_sb[:, j, :], start=(j == 0 and m == 0),
                                              stop=(j == NJ - 1 and m == 1))
                mm.then_inc(sems["dn_mm"], 1)

            guard_flag = []

            def attend(i, guarded):
                if active(i - 1):
                    scores(i - 1, 0, guarded)
                    scores(i - 1, 1, guarded)
                if active(i):
                    project(i)
                if active(i - 1):
                    for n in range(3):
                        scores(i - 1, n + 2, guarded)
                        products(i - 1, n)
                if active(i - 3):
                    ffn_up(i - 3, i, 0)
                if active(i - 1):
                    scores(i - 1, 5, guarded)
                    products(i - 1, 3)
                    scores(i - 1, 6, guarded)
                    products(i - 1, 4)
                    scores(i - 1, 7, guarded)
                    products(i - 1, 5)
                    attention_to_tokens(i - 1, 0)
                if active(i - 3):
                    ffn_up(i - 3, i, 1)
                if active(i - 1):
                    products(i - 1, 6)
                    products(i - 1, 7)
                if active(i - 3):
                    ffn_up(i - 3, i, 2)
                if active(i - 1):
                    attention_to_tokens(i - 1, 1)
                if active(i - 2):
                    mixed_to_tokens(i - 2)
                if active(i - 1):
                    attention_to_channels(i - 1)
                if active(i - 3):
                    ffn_up(i - 3, i, 3)

            def step(i):
                if isinstance(i, int) and i == 1:
                    pe.wait_ge(params_in, PARAMS)
                    pe.wait_ge(consts_done, 7)
                    pe.wait_ge(setup_dve, MIXER_IN)
                    guard_flag.append(pe.value_load(guard[0:1, 0:1], min_val=0, max_val=1))
                if isinstance(i, int) and i == 3:
                    pe.wait_ge(signs_done, 1 + NJ)
                if active(i - 1):
                    heads_to_rows(i - 1)
                if active(i - 4):
                    ffn_down(i - 4, 0)
                if active(i - 3):
                    x2_to_channels(i - 3, i)
                if active(i - 4):
                    ffn_down(i - 4, 1)
                if active(i - 2):
                    x1_to_channels(i - 2)
                if isinstance(i, int) and i == 1:
                    pe.wait_ge(consts_done, 13)
                if not active(i - 1):
                    attend(i, False)
                else:
                    with pe.If(guard_flag[0]):
                        row_scores(i - 1)
                        attend(i, True)
                    with pe.Else():
                        attend(i, False)
                if active(i - 1):
                    project_out(i - 1)

            pipeline(pe, step)

        @block.scalar
        def _(act):
            nc.scalar.preload_act_table_set("natural_log_exp_and_others")

            def mixer_constants():
                act.wait_ge(params_in, PARAMS)
                nc.scalar.activation(tdec2[:], tdec[:], ACT.Exp).then_inc(setup_act, 1)
                act.wait_ge(setup_act, 1)
                nc.scalar.activation(tdec[:], tdec2[:], ACT.Exp, scale=-1.0).then_inc(setup_act, 1)

            def mixer_weights():
                act.wait_ge(setup_dve, MIXER_IN + 2)
                nc.scalar.activation(e_state[:], u_pos[:], ACT.Exp, scale=-1.0).then_inc(setup_act, 1)
                nc.scalar.activation(e_now[:], u_neg[:], ACT.Exp).then_inc(setup_act, 1)

            def signs():
                act.wait_ge(ffn_in, 32)
                nc.scalar.activation(up_sb[:], up_f[:], ACT.Sign).then_inc(signs_done, 1)
                nc.scalar.activation(dn_f[:], dn_f[:], ACT.Sign).then_inc(setup_act, 1)

            def to_rows(p):
                done(act, "kT_tr", p)
                freed(act, "scores_mm", p)
                nc.scalar.activation(kT_sb[:], bank[4].bitcast(F16)[:, 0:512].rearrange("p (t b s) -> p t b s", t=T, b=2),
                                     ACT.Copy).then_inc(sems["kT_out"], 1)
                done(act, "qT_tr", p)
                nc.scalar.activation(qT_sb[:, 0], bank[0].bitcast(F16)[:].rearrange("p (b s) -> p b s", b=QBLOCKS),
                                     ACT.Copy).then_inc(sems["q0_out"], 1)

            def exps(p, *ns):
                for n in ns:
                    done(act, "scores_mm", p, n + 1)
                    if n >= KVH:
                        done(act, "pv_mm", p, n - KVH + 1)
                    else:
                        freed(act, "pv_mm", p, k=n + KVH + 1)
                    nc.scalar.activation(probs[:, n % KVH].rearrange("p a b -> p (a b)"), ring[n % 2][:], ACT.Exp)\
                        .then_inc(sems["probs_done"], 1)

            def take_products(p, t):
                done(act, "pv_mm", p, KVH * (t + 1))
                freed(act, "un_tr", p, k=t + 1)
                nc.scalar.activation(att_un[:, t].rearrange("p j s -> p (j s)"), bank[4 - 2 * t][:], ACT.Copy)\
                    .then_inc(sems["un_out"], 1)

            def relu(p, n):
                if n == 0:
                    freed(act, "lo2_done", p)
                    freed(act, "hidlo_done", p)
                    freed(act, "dn_mm", p)
                done(act, "up_mm", p, n + 1)
                for j in (2 * n, 2 * n + 1):
                    nc.scalar.activation(hid[:, j, :], bank[3 * (n % 2)][:, (j % 2) * T * S:(j % 2 + 1) * T * S],
                                         ACT.Relu, scale=ups_man[:, j:j + 1]).then_inc(sems["hid_done"], 1)

            def high_bits(p, n):
                done(act, "hid_done", p, 2 * n + 2)
                nc.scalar.activation(hid_hi[:, 2 * n:2 * n + 2], hid[:, 2 * n:2 * n + 2], ACT.Copy)\
                    .then_inc(sems["hidhi_done"], 1)

            def step(i):
                if active(i - 1):
                    to_rows(i - 1)
                if isinstance(i, int) and i == 1:
                    mixer_weights()
                    signs()
                if active(i - 3):
                    done(act, "x2T_tr", i - 3)
                    freed(act, "up_mm", i - 3)
                    nc.scalar.activation(x2hi[:].rearrange("p c t s -> p (c t s)"), bank[4][:], ACT.Copy)\
                        .then_inc(sems["x2hi_done"], 1)
                if active(i - 2):
                    done(act, "x1T_tr", i - 2)
                    freed(act, "ratio_done", i - 2)
                    for c in range(NC):
                        nc.scalar.activation(ke[:, 1, c], bank[5][:, c * T * S:(c + 1) * T * S]
                                             .rearrange("p (t s) -> p t s", t=T), ACT.Exp, bias=ln_max[:, 0:1])\
                            .then_inc(sems["ek_done"], 1)
                if active(i - 1):
                    exps(i - 1, 0, 1, 2)
                if active(i):
                    done(act, "qk_out", i)
                    freed(act, "ssum_done", i)
                    nc.scalar.activation(sq[:], qk[:], ACT.Square).then_inc(sems["sq_done"], 1)
                if active(i - 1):
                    exps(i - 1, 3)
                if active(i - 1):
                    exps(i - 1, 4)
                if active(i - 2):
                    done(act, "ratio_done", i - 2)
                    nc.scalar.activation(lnden[:], ratio[:, 1], ACT.Ln).then_inc(sems["ln_done"], 1)
                    done(act, "ln_done", i - 2)
                    freed(act, "guess_done", i - 2)
                    nc.scalar.activation(rec0[:], lnden[:], ACT.Exp, scale=-1.0).then_inc(sems["rec0_done"], 1)
                if active(i - 1):
                    exps(i - 1, 5)
                if active(i - 1):
                    take_products(i - 1, 0)
                if active(i - 1):
                    exps(i - 1, 6)
                if active(i):
                    done(act, "msq_done", i)
                    nc.scalar.activation(lnms[:], msq[:], ACT.Ln).then_inc(sems["ln_rms"], 1)
                    done(act, "ln_rms", i)
                    freed(act, "ny0_done", i)
                    nc.scalar.activation(y0[:], lnms[:], ACT.Exp, scale=-0.5).then_inc(sems["y0_done"], 1)
                if active(i - 1):
                    exps(i - 1, 7)
                if active(i - 3):
                    relu(i - 3, 0)
                if active(i - 1):
                    take_products(i - 1, 1)
                if active(i - 3):
                    relu(i - 3, 1)
                    high_bits(i - 3, 0)
                    relu(i - 3, 2)
                if active(i - 1):
                    done(act, "attT_tr", i - 1)
                    freed(act, "wo_mm", i - 1)
                    nc.scalar.activation(attT_sb[:].rearrange("p c t s -> p (c t s)"), bank[4][:], ACT.Copy)\
                        .then_inc(sems["attT_out"], 1)
                if active(i):
                    done(act, "qn_done", i)
                    nc.scalar.activation(stack[:, :, :, 0, :].rearrange("p t h d -> p (t h) d"), qn[:], ACT.Copy)\
                        .then_inc(sems["hi_done"], 1)
                if active(i - 3):
                    high_bits(i - 3, 1)
                    relu(i - 3, 3)
                if active(i):
                    if active(i - 1):
                        done(act, "pv_mm", i - 1)
                    else:
                        act.wait_ge(consts_done, 5)
                    done(act, "v_out", i)
                    nc.scalar.activation(v_sb[:, :, :, 0:HD], v_new[:], ACT.Copy).then_inc(sems["v_ready"], 1)
                if active(i - 3):
                    high_bits(i - 3, 2)
                    high_bits(i - 3, 3)
                if isinstance(i, int) and i == 0:
                    mixer_constants()

            pipeline(act, step)

        @block.gpsimd
        def _(pool):
            nc.gpsimd.memset(half_neg[:], -0.5).then_inc(consts_done, 1)
            nc.gpsimd.memset(ln_max[:], -LN_MAX).then_inc(consts_done, 1)
            nc.gpsimd.memset(v_sb[:], 1.0).then_inc(consts_done, 1)
            nc.gpsimd.memset(dec_sb[:], 1.0).then_inc(consts_done, 1)
            nc.gpsimd.memset(state[:], 0.0).then_inc(consts_done, 1)
            pool.wait_ge(consts_done, 5)

            def inverse_root(n, p):
                done(pool, f"ag{n + 1}", p)
                alone(pool)
                nc.gpsimd.tensor_scalar(veps[n][:], mv[n][:, :, 1], LN_EPS, 1.0, ALU.add, ALU.mult)\
                    .then_inc(sems[f"ve{n + 1}"], 1)
                done(pool, f"ve{n + 1}", p)
                nc.gpsimd.tensor_tensor(rstd[n][:], veps[n][:], half_neg[:, 0:T], ALU.pow)\
                    .then_inc(sems[f"rs{n + 1}"], 1)

            def low_bits(p, n):
                done(pool, "hidhi_done", p, n + 1)
                nc.gpsimd.tensor_tensor(hid_lo[:, 2 * n:2 * n + 2], hid[:, 2 * n:2 * n + 2],
                                        hid_hi[:, 2 * n:2 * n + 2], ALU.subtract).then_inc(sems["hidlo_done"], 1)

            def attention_constants():
                pool.wait_ge(params_in, PARAMS)
                nc.gpsimd.tensor_copy(id_h[:], id_f[:]).then_inc(consts_done, 1)
                nc.gpsimd.tensor_copy(id_b[:], id_f[:]).then_inc(consts_done, 1)
                nc.gpsimd.memset(mask_f[:], 0.0).then_inc(consts_done, 1)
                nc.gpsimd.memset(maskq_f[:], 0.0).then_inc(consts_done, 1)
                pool.wait_ge(consts_done, 9)
                for m, sign in ((mask_f, 1), (maskq_f, -1)):
                    nc.gpsimd.affine_select(out=m[:], in_=m[:], compare_op=ALU.is_ge, fill=pool.to_reg(MASKED), base=0,
                                            pattern=[[0, REP], [sign, S]], channel_multiplier=-sign)\
                        .then_inc(consts_done, 1)
                pool.wait_ge(consts_done, 11)
                nc.gpsimd.tensor_copy(mask_sb[:], mask_f[:]).then_inc(consts_done, 1)
                nc.gpsimd.tensor_copy(maskq_sb[:], maskq_f[:]).then_inc(consts_done, 1)

            def rope_products(p):
                if first(p):
                    pool.wait_ge(norm_in, NORM_IN)
                done(pool, "qk_out", p)
                freed(pool, "qn_done", p)
                half = HD // 2
                c = cos_sb[:].unsqueeze(1).to_broadcast([128, T * NQK, HD])
                if not first(p):
                    nc.gpsimd.tensor_tensor(rope_a[:], qk[:], c, ALU.mult).then_inc(sems["rope_done"], 1)
                for to, of in ((0, half), (half, 0)):
                    s = sin_sb[:, to:to + half].unsqueeze(1).to_broadcast([128, T * NQK, half])
                    nc.gpsimd.tensor_tensor(rope_b[:, :, to:to + half], qk[:, :, of:of + half], s, ALU.mult)\
                        .then_inc(sems["rope_done"], 1)

            def step(i):
                if active(i - 2):
                    inverse_root(0, i - 2)
                if active(i - 1):
                    done(pool, "x_in", i - 1)
                    freed(pool, "r1_done", i - 1)
                    nc.gpsimd.tensor_tensor(xb_sb[:], x_sb[:], bo_b[:].unsqueeze(1).to_broadcast([128, T, D]), ALU.add)\
                        .then_inc(sems["xb_done"], 1)
                if active(i - 2):
                    p = i - 2
                    if isinstance(i, int) and i == 2:
                        pool.wait_ge(setup_act, 4)
                    done(pool, "ctx_in", p)
                    done(pool, "ek_done", p)
                    nc.gpsimd.tensor_tensor(ke[:, 0], ke[:, 1], ctxT_sb[:], ALU.mult).then_inc(sems["kv_done"], 1)
                    done(pool, "kv_done", p)
                    freed(pool, "ratio_done", p)
                    for c in range(NC):
                        alone(pool)
                        nc.gpsimd.tensor_scalar(now[:, :, c].rearrange("p a t s -> p a (t s)"),
                                                ke[:, :, c].rearrange("p a t s -> p a (t s)"),
                                                e_now[:, c:c + 1], 1.0, ALU.mult, ALU.mult).then_inc(sems["now_done"], 1)
                if active(i - 4):
                    inverse_root(2, i - 4)
                if active(i):
                    rope_products(i)
                if active(i - 2):
                    done(pool, "rec0_done", i - 2)
                    freed(pool, "ny_done", i - 2)
                    nc.gpsimd.tensor_tensor(newt[:], ratio[:, 1], rec0[:], ALU.mult).then_inc(sems["guess_done"], 1)
                    nc.gpsimd.tensor_tensor(guess[:], ratio[:, 0], rec0[:], ALU.mult).then_inc(sems["guess_done"], 1)
                if active(i):
                    if not first(i):
                        done(pool, "rope_done", i)
                        nc.gpsimd.tensor_tensor(rot[:], rope_a[:], rope_b[:], ALU.add).then_inc(sems["rot_done"], 1)
                if isinstance(i, int) and i == 0:
                    attention_constants()
                if active(i - 3):
                    low_bits(i - 3, 0)
                if active(i - 2):
                    inverse_root(1, i - 2)
                if active(i - 3):
                    low_bits(i - 3, 1)
                    low_bits(i - 3, 3)

            pipeline(pool, step)

        @block.vector
        def _(dve):
            dve.wait_ge(project_in, PROJECT_IN)

            def gains_constants():
                nc.vector.memset(gain_b[:], -0.5).then_inc(setup_dve, 1)
                dve.wait_ge(norm_in, NORM_IN)
                dve.wait_ge(setup_dve, 1)
                nc.vector.tensor_scalar(gain_b[:, :, 0:H], gain_in[:], -0.5 * HD ** -0.5, None, ALU.mult)\
                    .then_inc(setup_dve, 1)
                nc.vector.tensor_tensor(gain_sq[:], gain_in[:, 0], gain_in[:, 0], ALU.mult).then_inc(setup_dve, 1)
                dve.wait_ge(setup_dve, 3)
                nc.vector.tensor_reduce(gain_top[:], gain_sq[:], AX_X, ALU.max).then_inc(setup_dve, 1)
                dve.wait_ge(setup_dve, 4)
                nc.vector.tensor_scalar(guard[:], gain_top[:], GAIN_LIMIT * GAIN_LIMIT, None, ALU.is_gt)\
                    .then_inc(setup_dve, 1)
                dve.wait_ge(setup_dve, 5)

            guard_flag = []

            def row_maxima(p):
                for n in range(T * KVH):
                    done(dve, "rows_mm", p, n + 1)
                    nc.vector.tensor_reduce(row_max[:, n], bank[2][:].rearrange("p (j s) -> p j s", j=REP), AX_X,
                                            ALU.max).then_inc(sems["rows_max"], 1)
                done(dve, "max_tr", p)
                freed(dve, "scores_mm", p)
                nc.vector.tensor_scalar(shift[:], bank[2][0:T * H, 0:S], -1.0, None, ALU.mult)\
                    .then_inc(sems["shift_done"], 1)

            def mixer_constants():
                dve.wait_ge(params_in, PARAMS)
                nc.vector.tensor_scalar(u_pos[:], tfirst[:], 0.0, None, ALU.max).then_inc(setup_dve, 1)
                nc.vector.tensor_scalar(u_neg[:], tfirst[:], 0.0, None, ALU.min).then_inc(setup_dve, 1)
                dve.wait_ge(consts_done, 5)
                nc.vector.tensor_scalar(ups_pow[:].bitcast(I32), ups_sb[:].bitcast(I32), 0x7F800000, None,
                                        ALU.bitwise_and).then_inc(setup_dve, 1)
                nc.vector.tensor_scalar(ups_man[:].bitcast(I32), ups_sb[:].bitcast(I32), -0x7F800001, 0x3F800000,
                                        ALU.bitwise_and, ALU.bitwise_or).then_inc(setup_dve, 1)
                nc.vector.tensor_scalar(dsc_b[:], dsc_b[:], osc_b[:, 0:1], None, ALU.mult).then_inc(setup_dve, 1)
                dve.wait_ge(setup_act, 2)
                dve.wait_ge(setup_dve, MIXER_IN + 5)
                for c in range(NC):
                    nc.vector.tensor_scalar(dec_sb[:, :, c].rearrange("p a t s -> p a (t s)"),
                                            dec_sb[:, :, c].rearrange("p a t s -> p a (t s)"),
                                            tdec[:, c:c + 1], None, ALU.mult).then_inc(setup_dve, 1)
                dve.wait_ge(setup_dve, MIXER_IN + 7)
                nc.vector.memset(dec_sb[:].rearrange("p a c t s -> p (a c t) s")[:, :, 0:1], 0.0).then_inc(setup_dve, 1)
                dve.wait_ge(setup_dve, MIXER_IN + 8)

            def attend_norm(p, t):
                done(dve, "un_tr", p, t + 1)
                o = bank[4 - 2 * t][:].rearrange("p (j g d) -> p j g d", j=REP, g=KVH)
                nc.vector.reciprocal(prec[:, t].rearrange("p (j g) -> p j g", j=REP), o[:, :, :, HD])\
                    .then_inc(sems["prec_done"], 1)
                done(dve, "prec_done", p, t + 1)
                freed(dve, "attT_tr", p)
                nc.vector.tensor_tensor(att[:, t].rearrange("p (g j) d -> p j g d", g=KVH), o[:, :, :, 0:HD],
                                        prec[:, t].rearrange("p (j g) -> p j g", j=REP).unsqueeze(3)
                                        .to_broadcast([128, REP, KVH, HD]), ALU.mult).then_inc(sems["att_done"], 1)

            def moments(n, p, rows):
                for t in range(T):
                    nc.vector.bn_stats(stats[n][:, t], rows[:, t, :]).then_inc(sems[f"bn{n + 1}"], 1)
                for t in range(T):
                    done(dve, f"bn{n + 1}", p, t + 1)
                    alone(dve)
                    nc.vector.bn_aggr(mv[n][:, t], stats[n][:, t]).then_inc(sems[f"ag{n + 1}"], 1)

            def normed(n, p, rows, to, name):
                done(dve, f"rs{n + 1}", p)
                for t in range(T):
                    nc.vector.tensor_scalar(to[:, t], rows[:, t, :], mv[n][:, t, 0:1], rstd[n][:, t:t + 1],
                                            ALU.subtract, ALU.mult).then_inc(sems[name], 1)

            W = NC * T * S

            def scan(p):
                done(dve, "kv_done", p)
                nc.vector.tensor_tensor_scan(state[:, 1:2 * W + 1], dec_sb[:].rearrange("p a c t s -> p (a c t s)"),
                                             ke[:].rearrange("p a c t s -> p (a c t s)"), 0.0, ALU.mult, ALU.add)\
                    .then_inc(sems["scan_done"], 1)

            def mix(p):
                done(dve, "scan_done", p)
                nc.vector.tensor_copy(state[:, 0:2 * W].rearrange("p (n s) -> p n s", s=S)[:, :, 0:1],
                                      ke[:].rearrange("p a c t s -> p (a c t) s")[:, :, 0:1]).then_inc(sems["fix_done"], 1)
                done(dve, "fix_done", p)
                done(dve, "now_done", p)
                for c in range(NC):
                    nc.vector.scalar_tensor_tensor(
                        ratio[:, :, c].rearrange("p a t s -> p a (t s)"),
                        state[:, 0:2 * W].rearrange("p (a c n) -> p a c n", a=2, c=NC)[:, :, c, :],
                        e_state[:, c:c + 1], now[:, :, c].rearrange("p a t s -> p a (t s)"),
                        ALU.mult, ALU.add).then_inc(sems["ratio_done"], 1)

            def down_weights():
                dve.wait_ge(setup_act, 5)
                for j in range(NJ):
                    nc.vector.tensor_scalar(dn_sb[:, j], dn_f[:, j], ups_pow[:, j:j + 1], None, ALU.mult)\
                        .then_inc(signs_done, 1)

            def newton_rms(p):
                done(dve, "y0_done", p)
                nc.vector.tensor_tensor(ysq[:], y0[:], y0[:], ALU.mult).then_inc(sems["ysq_done"], 1)
                done(dve, "ysq_done", p)
                nc.vector.tensor_tensor(vy[:], ysq[:], msq[:], ALU.mult).then_inc(sems["vy_done"], 1)
                done(dve, "vy_done", p)
                nc.vector.scalar_tensor_tensor(ny0[:], vy[:], 3.0, y0[:], ALU.subtract, ALU.mult)\
                    .then_inc(sems["ny0_done"], 1)
                done(dve, "ny0_done", p)
                nc.vector.tensor_tensor(rscale[:], ny0[:], gain_b[:].rearrange("p t h -> p (t h)"), ALU.mult)\
                    .then_inc(sems["rscale_done"], 1)

            def low_bits(p):
                n = 2
                done(dve, "hidhi_done", p, n + 1)
                nc.vector.tensor_tensor(hid_lo[:, 2 * n:2 * n + 2], hid[:, 2 * n:2 * n + 2],
                                        hid_hi[:, 2 * n:2 * n + 2], ALU.subtract).then_inc(sems["lo2_done"], 1)

            def fill_stack(p):
                done(dve, "hi_done", p)
                nc.vector.tensor_tensor(stack[:, :, :, 1, :].rearrange("p t h d -> p (t h) d"), qn[:],
                                        stack[:, :, :, 0, :].rearrange("p t h d -> p (t h) d"), ALU.subtract)\
                    .then_inc(sems["lo_done"], 1)
                done(dve, "lo_done", p)
                nc.vector.tensor_copy(stack[:, :, 0:H, 2:4, :].rearrange("p t h r d -> p t h (r d)"),
                                      stack[:, :, 0:H, 0:2, :].rearrange("p t h r d -> p t h (r d)"))\
                    .then_inc(sems["stack_done"], 1)
                for to, of in ((2, 1), (3, 0)):
                    nc.vector.tensor_copy(stack[:, :, H:NQK, to, :], stack[:, :, H:NQK, of, :])\
                        .then_inc(sems["stack_done"], 1)

            z = bank[5][:].rearrange("p (t d) -> p t d", t=T)

            def step(i):
                if active(i - 2):
                    p = i - 2
                    done(dve, "wo_mm", p)
                    done(dve, "xb_done", p)
                    nc.vector.tensor_tensor(r1[:].rearrange("p t d -> p (t d)"), bank[2][:],
                                            xb_sb[:].rearrange("p t d -> p (t d)"), ALU.add).then_inc(sems["r1_done"], 1)
                if active(i - 4):
                    low_bits(i - 4)
                if active(i - 2):
                    done(dve, "r1_done", i - 2)
                    moments(0, i - 2, r1)
                if active(i - 1):
                    p = i - 1
                    done(dve, "qT_tr", p, 1)
                    freed(dve, "scores_mm", p)
                    nc.vector.tensor_copy(qT_sb[:, 1].rearrange("p b s -> p (b s)"), bank[3].bitcast(F16)[:])\
                        .then_inc(sems["q1_out"], 1)
                if isinstance(i, int) and i == 1:
                    mixer_constants()
                    down_weights()
                    guard_flag.append(dve.value_load(guard[0:1, 0:1], min_val=0, max_val=1))
                if active(i - 2):
                    freed(dve, "x1T_tr", i - 2)
                    normed(0, i - 2, r1, x1, "x1_done")
                if active(i - 3):
                    done(dve, "x2hi_done", i - 3)
                    nc.vector.tensor_tensor(x2lo[:].rearrange("p c t s -> p (c t s)"), bank[4][:],
                                            x2hi[:].rearrange("p c t s -> p (c t s)"), ALU.subtract)\
                        .then_inc(sems["x2lo_done"], 1)
                if active(i - 1):
                    with dve.If(guard_flag[0]):
                        row_maxima(i - 1)
                if active(i - 4):
                    p = i - 4
                    done(dve, "dn_mm", p)
                    freed(dve, "r3_done", p)
                    nc.vector.tensor_tensor(o3[:], bank[1][:].rearrange("p (t d) -> p t d", t=T),
                                            dsc_b[:].unsqueeze(1).to_broadcast([128, T, D]), ALU.mult)\
                        .then_inc(sems["o3_done"], 1)
                    done(dve, "o3_done", p)
                    done(dve, "kept", p)
                    nc.vector.tensor_tensor(r3[:], o3[:], x2_keep[:], ALU.add).then_inc(sems["r3_done"], 1)
                    done(dve, "r3_done", p)
                    moments(2, p, r3)
                if active(i - 2):
                    scan(i - 2)
                if active(i):
                    done(dve, "qkv_mm", i)
                    for t in range(T):
                        ins = nc.vector.tensor_tensor(qk[:, t * NQK:(t + 1) * NQK, :].rearrange("p h d -> p (h d)"),
                                                      bank[3 * t][:, 0:NQK * HD], bqk_b[:, 0:NQK * HD], ALU.add)
                    ins.then_inc(sems["qk_out"], 1)
                    freed(dve, "v_ready", i)
                    for t in range(T):
                        ins = nc.vector.tensor_tensor(v_new[:, t],
                                                      bank[3 * t][:, NQK * HD:E].rearrange("p (g d) -> p g d", g=KVH),
                                                      bqk_b[:, NQK * HD:E].rearrange("p (g d) -> p g d", g=KVH), ALU.add)
                    ins.then_inc(sems["v_out"], 1)
                if isinstance(i, int) and i == 0:
                    dve.wait_ge(norm_in, NORM_IN)
                    done(dve, "qk_out", i)
                    nc.vector.tensor_tensor(rope_a[:], qk[:], cos_sb[:].unsqueeze(1).to_broadcast([128, T * NQK, HD]),
                                            ALU.mult).then_inc(sems["rope_done"], 1)
                if active(i - 2):
                    mix(i - 2)
                if active(i):
                    done(dve, "sq_done", i)
                    nc.vector.tensor_reduce(ssum[:], sq[:], AX_X, ALU.add).then_inc(sems["ssum_done"], 1)
                    done(dve, "ssum_done", i)
                    nc.vector.tensor_scalar(msq[:], ssum[:], 1.0 / HD, RMS_EPS, ALU.mult, ALU.add)\
                        .then_inc(sems["msq_done"], 1)
                if active(i - 4):
                    freed(dve, "stored", i - 4)
                    normed(2, i - 4, r3, outb, "out_done")
                if isinstance(i, int) and i == 0:
                    gains_constants()
                if active(i):
                    newton_rms(i)
                if isinstance(i, int) and i == 0:
                    done(dve, "rope_done", i)
                    nc.vector.tensor_tensor(rot[:], rope_a[:], rope_b[:], ALU.add).then_inc(sems["rot_done"], 1)
                if active(i - 1):
                    attend_norm(i - 1, 0)
                if active(i - 2):
                    p = i - 2
                    done(dve, "guess_done", p)
                    nc.vector.scalar_tensor_tensor(ny[:], newt[:], 2.0, guess[:], ALU.subtract, ALU.mult)\
                        .then_inc(sems["ny_done"], 1)
                if active(i - 2):
                    p = i - 2
                    done(dve, "ny_done", p)
                    freed(dve, "zT_tr", p)
                    nc.vector.tensor_tensor(zT[:].rearrange("p c t s -> p (c t s)"), bank[5][:],
                                            ny[:].rearrange("p c t s -> p (c t s)"), ALU.subtract)\
                        .then_inc(sems["z_done"], 1)
                if active(i - 1):
                    attend_norm(i - 1, 1)
                if active(i):
                    done(dve, "rscale_done", i)
                    done(dve, "rot_done", i)
                    nc.vector.tensor_tensor(qn[:], rot[:], rscale[:].unsqueeze(2).to_broadcast([128, T * NQK, HD]),
                                            ALU.mult).then_inc(sems["qn_done"], 1)
                if active(i - 2):
                    done(dve, "zT_tr", i - 2)
                    moments(1, i - 2, z)
                if active(i):
                    fill_stack(i)
                if active(i - 2):
                    freed(dve, "x2T_tr", i - 2)
                    freed(dve, "kept", i - 2)
                    normed(1, i - 2, z, x2, "x2_done")

            pipeline(dve, step)


def kernel(x, ctx_2048, L0_attn_Wq, L0_attn_bq, L0_attn_Wk, L0_attn_bk, L0_attn_Wv, L0_attn_bv, L0_attn_Wo,
           L0_attn_bo, L0_attn_q_gain, L0_xattn_time_decay, L0_xattn_time_first, L0_ffn_up_weight,
           L0_ffn_down_weight, L0_ffn_up_scale, L0_ffn_down_scale, L0_ffn_output_scale):
    import concourse.bacc as bacc
    from concourse.bass_utils import run_bass_kernel_spmd

    def a(v):
        return np.asarray(v)

    order = np.arange(H).reshape(2, 2, REP).transpose(0, 2, 1).reshape(H)
    wq = a(L0_attn_Wq).reshape(H, HD, D)[order].reshape(D, D)
    bq = a(L0_attn_bq).reshape(H, HD)[order].reshape(D)

    def chunked(w):
        return np.ascontiguousarray(w.reshape(-1, 128, w.shape[1]).transpose(1, 0, 2))

    def to_channels(v):
        return np.ascontiguousarray(a(v).reshape(PAIRS, T, S, NC, 128).transpose(0, 4, 3, 1, 2))

    inv_freq = (np.float32(1.0) / np.float32(10000.0) ** (np.arange(0, HD, 2, dtype=np.float32) / np.float32(HD)))
    freqs = np.outer(np.arange(S, dtype=np.float32), inv_freq.astype(np.float32)).astype(np.float32)
    cos, sin = np.cos(freqs), np.sin(freqs)

    arrays = {
        "x": np.ascontiguousarray(a(x).reshape(PAIRS, T, S, D).transpose(0, 2, 1, 3)),
        "xT": to_channels(x),
        "ctxT": to_channels(ctx_2048),
        "wqkv": chunked(np.concatenate([wq, a(L0_attn_Wk), a(L0_attn_Wv)]).T),
        "bqkv": np.concatenate([bq, a(L0_attn_bk), a(L0_attn_bv)]),
        "gains": a(L0_attn_q_gain)[order],
        "wo": chunked(a(L0_attn_Wo).T),
        "bo": a(L0_attn_bo),
        "decay_in": np.ascontiguousarray(a(L0_xattn_time_decay).reshape(NC, 128).T),
        "first_in": np.ascontiguousarray(a(L0_xattn_time_first).reshape(NC, 128).T),
        "up": chunked(a(L0_ffn_up_weight).T),
        "down": chunked(a(L0_ffn_down_weight).T),
        "up_s": np.ascontiguousarray(a(L0_ffn_up_scale).reshape(NJ, 128).T),
        "down_s": a(L0_ffn_down_scale),
        "out_s": a(L0_ffn_output_scale),
        "rope_cos": np.concatenate([cos, cos], 1).astype(np.float32),
        "rope_sin": np.concatenate([sin, -sin], 1).astype(np.float32),
        "ident_in": np.eye(128, dtype=np.float32),
    }
    nc = bacc.Bacc("TRN2", target_bir_lowering=False, num_devices=1)
    args = [nc.dram_tensor(f"{n}_dram", v.shape, F32, kind="ExternalInput").ap() for n, v in arrays.items()]
    result = nc.dram_tensor("out_dram", (PAIRS, S, T, D), F32, kind="ExternalOutput").ap()
    build(nc, *args, result)
    r = run_bass_kernel_spmd(nc, [{f"{n}_dram": v for n, v in arrays.items()}], core_ids=[0])
    got = r.results[0]["out_dram"]
    return np.ascontiguousarray(got.reshape(PAIRS, S, T, D).transpose(0, 2, 1, 3)).reshape(B, S, D)
```
